# Optimizing a Trainium2 kernel written in Bass

```python
import numpy as np
import jax
import jax.numpy as jnp

def _softmax(x, axis=-1):
    return jax.nn.softmax(x, axis=axis)
def _gelu(x):
    return jax.nn.gelu(x, approximate=True)
def _silu(x):
    return jax.nn.silu(x)
def _sigmoid(x):
    return jax.nn.sigmoid(x)
def _layernorm(x, axis=-1, eps=1e-5):
    m = jnp.mean(x, axis=axis, keepdims=True)
    v = jnp.var(x, axis=axis, keepdims=True)
    return (x - m) / jnp.sqrt(v + eps)
def _scatter_add(tgt, idx, src, axis=0):
    return tgt.at[idx].add(src)
def _segment_sum(src, seg, n):
    return jax.ops.segment_sum(src, seg, n)

kernel_name = 'mk_conv_seq_d2_conv_nhwc192_af98aa'

def setup_inputs(seed: int = 0):
    np.random.seed(seed)
    _w = jnp.asarray
    def _rec_inputs():
        import jax
        import jax.numpy as jnp
        _gk = jax.random.key(seed)
        x = -0.0001538 + 1 * jax.random.normal(jax.random.fold_in(_gk, 1), (8, 64, 64, 192), jnp.float32)
        return x
    x = _rec_inputs()
    def _L0_conv_setup():
        import jax, jax.numpy as jnp
        import numpy as np
        import math
        B, H, W, CIN = (8, 64, 64, 192)
        INNER, K, N, P = (384, 2, 32, 64)
        NHK = INNER // P
        NH = K * NHK
        HID = 4 * CIN

        def _silu(v):
            return v * jax.nn.sigmoid(v)
        key = jax.random.key(seed)
        ks = jax.random.split(key, 12)
        x = jax.random.normal(ks[0], (B, H, W, CIN), jnp.float32)
        W_in = jax.random.normal(ks[1], (2 * INNER, CIN), jnp.float32) * 0.02
        conv_w = jax.random.normal(ks[2], (INNER, 1, 3, 3), jnp.float32) * 0.1
        conv_b = jnp.zeros((INNER,), jnp.float32)
        x_proj_weight = jax.random.normal(ks[3], (K, 2 * N + NHK, INNER), jnp.float32) * 0.02
        A_logs = jnp.log(jax.random.uniform(ks[4], (NH,), jnp.float32, 1.0, 16.0))
        Ds = jnp.ones((NH,), jnp.float32)
        u = jax.random.uniform(ks[5], (NH,), jnp.float32)
        dt = jnp.exp(u * (math.log(0.1) - math.log(0.001)) + math.log(0.001))
        dt = jnp.clip(dt, 0.0001, None)
        dt_bias = dt + jnp.log(-jnp.expm1(-dt))
        init_states = jnp.zeros((NH, P, N), jnp.float32)
        W_out = jax.random.normal(ks[6], (CIN, INNER), jnp.float32) * 0.02
        W1 = jax.random.normal(ks[7], (HID, CIN), jnp.float32) * 0.02
        b1 = jnp.zeros((HID,), jnp.float32)
        W2 = jax.random.normal(ks[8], (CIN, HID), jnp.float32) * 0.02
        b2 = jnp.zeros((CIN,), jnp.float32)
        return dict(x=x, W_in=W_in, conv_w=conv_w, conv_b=conv_b, x_proj_weight=x_proj_weight, A_logs=A_logs, Ds=Ds, dt_bias=dt_bias, init_states=init_states, W_out=W_out, W1=W1, b1=b1, W2=W2, b2=b2)
    _L0_conv_all = _L0_conv_setup()
    _L0_conv_in = {k: v for k, v in _L0_conv_all.items() if k in ('W_in', 'conv_w', 'conv_b', 'x_proj_weight', 'A_logs', 'Ds', 'dt_bias', 'init_states', 'W_out', 'W1', 'b1', 'W2', 'b2', )}
    del _L0_conv_all

    def _L1_conv_setup():
        import jax, jax.numpy as jnp
        import numpy as np
        from jax import lax
        EPS = 1e-05
        Bq, Hq, Wq, Cq = (8, 56, 56, 192)
        D_HALF, D_INNER, D_STATE, DT_RANK, K = (96, 192, 16, 6, 4)

        def _bn(x, g, b, m, v):
            return (x - m) * (g * lax.rsqrt(v + EPS)) + b

        def _ln(x, g, b):
            mu = jnp.mean(x, -1, keepdims=True)
            var = jnp.mean((x - mu) ** 2, -1, keepdims=True)
            return (x - mu) * lax.rsqrt(var + EPS) * g + b

        def _conv(x, w, b, groups=1):
            y = lax.conv_general_dilated(x, w, (1, 1), 'SAME', dimension_numbers=('NHWC', 'HWIO', 'NHWC'), feature_group_count=groups)
            return y + b

        def _forward(x, bn1_g, bn1_b, bn1_m, bn1_v, bn2_g, bn2_b, bn2_m, bn2_v, bn3_g, bn3_b, bn3_m, bn3_v, conv1_w, conv1_b, conv2_w, conv2_b, conv3_w, conv3_b, ln_g, ln_b, in_proj_w, conv2d_w, conv2d_b, x_proj_w, dt_proj_w, dt_proj_b, A_logs, Ds, out_norm_g, out_norm_b, out_proj_w):
            B, H, W, C = x.shape
            L = H * W
            xl, xr = (x[..., :D_HALF], x[..., D_HALF:])
            y = _bn(xl, bn1_g, bn1_b, bn1_m, bn1_v)
            y = _conv(y, conv1_w, conv1_b)
            y = jax.nn.relu(_bn(y, bn2_g, bn2_b, bn2_m, bn2_v))
            y = _conv(y, conv2_w, conv2_b)
            y = jax.nn.relu(_bn(y, bn3_g, bn3_b, bn3_m, bn3_v))
            xl_out = jax.nn.relu(_conv(y, conv3_w, conv3_b))
            xr_n = _ln(xr, ln_g, ln_b)
            xz = jnp.einsum('bhwc,ec->bhwe', xr_n, in_proj_w)
            xi, z = (xz[..., :D_INNER], xz[..., D_INNER:])
            xi = jax.nn.silu(_conv(xi, conv2d_w, conv2d_b, groups=D_INNER))
            xc = jnp.transpose(xi, (0, 3, 1, 2))
            x_hw = xc.reshape(B, D_INNER, L)
            x_wh = jnp.transpose(xc, (0, 1, 3, 2)).reshape(B, D_INNER, L)
            x2 = jnp.stack([x_hw, x_wh], 1)
            xs4 = jnp.concatenate([x2, jnp.flip(x2, -1)], 1)
            x_dbl = jnp.einsum('bkdl,kcd->bkcl', xs4, x_proj_w)
            dts = x_dbl[:, :, :DT_RANK]
            Bs = x_dbl[:, :, DT_RANK:DT_RANK + D_STATE]
            Cs = x_dbl[:, :, DT_RANK + D_STATE:]
            delta = jax.nn.softplus(jnp.einsum('bkrl,kdr->bkdl', dts, dt_proj_w) + dt_proj_b[None, :, :, None])
            A = -jnp.exp(A_logs)

            def step(h, t):
                u_t, d_t, b_t, c_t = t
                h = jnp.exp(d_t[..., None] * A) * h + (d_t * u_t)[..., None] * b_t[:, :, None, :]
                return (h, jnp.einsum('bkdn,bkn->bkd', h, c_t))
            scan_in = (jnp.moveaxis(xs4, -1, 0), jnp.moveaxis(delta, -1, 0), jnp.moveaxis(Bs, -1, 0), jnp.moveaxis(Cs, -1, 0))
            h0 = jnp.zeros((B, K, D_INNER, D_STATE), x.dtype)
            _, ys = lax.scan(step, h0, scan_in)
            ys = jnp.moveaxis(ys, 0, -1) + Ds[None, :, :, None] * xs4

            def wh2hw(t):
                return jnp.transpose(t.reshape(B, D_INNER, W, H), (0, 1, 3, 2)).reshape(B, D_INNER, L)
            yv = ys[:, 0] + jnp.flip(ys[:, 2], -1) + wh2hw(ys[:, 1]) + wh2hw(jnp.flip(ys[:, 3], -1))
            yv = jnp.transpose(yv, (0, 2, 1)).reshape(B, H, W, D_INNER)
            yv = _ln(yv, out_norm_g, out_norm_b) * jax.nn.silu(z)
            xr_out = jnp.einsum('bhwe,ce->bhwc', yv, out_proj_w)
            fused = jnp.concatenate([xl_out, xr_out], -1)
            fused = jnp.swapaxes(fused.reshape(B, H, W, 2, C // 2), 3, 4).reshape(B, H, W, C)
            return fused + x
        key = jax.random.key(seed)
        ks = iter(jax.random.split(key, 64))

        def rn(shape, s=0.05):
            return jax.random.normal(next(ks), shape, jnp.float32) * s
        inp = {'x': jax.random.normal(next(ks), (Bq, Hq, Wq, Cq), jnp.float32)}
        for i in (1, 2, 3):
            inp[f'bn{i}_g'] = jnp.ones((D_HALF,), jnp.float32)
            inp[f'bn{i}_b'] = jnp.zeros((D_HALF,), jnp.float32)
            inp[f'bn{i}_m'] = rn((D_HALF,), 0.1)
            inp[f'bn{i}_v'] = 1.0 + jax.random.uniform(next(ks), (D_HALF,), jnp.float32) * 0.1
        inp['conv1_w'] = rn((3, 3, D_HALF, D_HALF))
        inp['conv1_b'] = rn((D_HALF,))
        inp['conv2_w'] = rn((3, 3, D_HALF, D_HALF))
        inp['conv2_b'] = rn((D_HALF,))
        inp['conv3_w'] = rn((1, 1, D_HALF, D_HALF))
        inp['conv3_b'] = rn((D_HALF,))
        inp['ln_g'] = jnp.ones((D_HALF,), jnp.float32)
        inp['ln_b'] = jnp.zeros((D_HALF,), jnp.float32)
        inp['in_proj_w'] = rn((2 * D_INNER, D_HALF))
        inp['conv2d_w'] = rn((3, 3, 1, D_INNER))
        inp['conv2d_b'] = rn((D_INNER,))
        inp['x_proj_w'] = rn((K, DT_RANK + 2 * D_STATE, D_INNER))
        inp['dt_proj_w'] = rn((K, D_INNER, DT_RANK))
        inp['dt_proj_b'] = rn((K, D_INNER))
        inp['A_logs'] = jnp.tile(jnp.log(jnp.arange(1, D_STATE + 1, dtype=jnp.float32))[None, None, :], (K, D_INNER, 1))
        inp['Ds'] = jnp.ones((K, D_INNER), jnp.float32)
        inp['out_norm_g'] = jnp.ones((D_INNER,), jnp.float32)
        inp['out_norm_b'] = jnp.zeros((D_INNER,), jnp.float32)
        inp['out_proj_w'] = rn((D_HALF, D_INNER))
        return inp
    _L1_conv_all = _L1_conv_setup()
    _L1_conv_in = {k: v for k, v in _L1_conv_all.items() if k in ('bn1_g', 'bn1_b', 'bn1_m', 'bn1_v', 'bn2_g', 'bn2_b', 'bn2_m', 'bn2_v', 'bn3_g', 'bn3_b', 'bn3_m', 'bn3_v', 'conv1_w', 'conv1_b', 'conv2_w', 'conv2_b', 'conv3_w', 'conv3_b', 'ln_g', 'ln_b', 'in_proj_w', 'conv2d_w', 'conv2d_b', 'x_proj_w', 'dt_proj_w', 'dt_proj_b', 'A_logs', 'Ds', 'out_norm_g', 'out_norm_b', 'out_proj_w', )}
    del _L1_conv_all

    return {
        "x": x,
        "L0_conv_W_in": _L0_conv_in["W_in"],
        "L0_conv_conv_w": _L0_conv_in["conv_w"],
        "L0_conv_conv_b": _L0_conv_in["conv_b"],
        "L0_conv_x_proj_weight": _L0_conv_in["x_proj_weight"],
        "L0_conv_A_logs": _L0_conv_in["A_logs"],
        "L0_conv_Ds": _L0_conv_in["Ds"],
        "L0_conv_dt_bias": _L0_conv_in["dt_bias"],
        "L0_conv_init_states": _L0_conv_in["init_states"],
        "L0_conv_W_out": _L0_conv_in["W_out"],
        "L0_conv_W1": _L0_conv_in["W1"],
        "L0_conv_b1": _L0_conv_in["b1"],
        "L0_conv_W2": _L0_conv_in["W2"],
        "L0_conv_b2": _L0_conv_in["b2"],
        "L1_conv_bn1_g": _L1_conv_in["bn1_g"],
        "L1_conv_bn1_b": _L1_conv_in["bn1_b"],
        "L1_conv_bn1_m": _L1_conv_in["bn1_m"],
        "L1_conv_bn1_v": _L1_conv_in["bn1_v"],
        "L1_conv_bn2_g": _L1_conv_in["bn2_g"],
        "L1_conv_bn2_b": _L1_conv_in["bn2_b"],
        "L1_conv_bn2_m": _L1_conv_in["bn2_m"],
        "L1_conv_bn2_v": _L1_conv_in["bn2_v"],
        "L1_conv_bn3_g": _L1_conv_in["bn3_g"],
        "L1_conv_bn3_b": _L1_conv_in["bn3_b"],
        "L1_conv_bn3_m": _L1_conv_in["bn3_m"],
        "L1_conv_bn3_v": _L1_conv_in["bn3_v"],
        "L1_conv_conv1_w": _L1_conv_in["conv1_w"],
        "L1_conv_conv1_b": _L1_conv_in["conv1_b"],
        "L1_conv_conv2_w": _L1_conv_in["conv2_w"],
        "L1_conv_conv2_b": _L1_conv_in["conv2_b"],
        "L1_conv_conv3_w": _L1_conv_in["conv3_w"],
        "L1_conv_conv3_b": _L1_conv_in["conv3_b"],
        "L1_conv_ln_g": _L1_conv_in["ln_g"],
        "L1_conv_ln_b": _L1_conv_in["ln_b"],
        "L1_conv_in_proj_w": _L1_conv_in["in_proj_w"],
        "L1_conv_conv2d_w": _L1_conv_in["conv2d_w"],
        "L1_conv_conv2d_b": _L1_conv_in["conv2d_b"],
        "L1_conv_x_proj_w": _L1_conv_in["x_proj_w"],
        "L1_conv_dt_proj_w": _L1_conv_in["dt_proj_w"],
        "L1_conv_dt_proj_b": _L1_conv_in["dt_proj_b"],
        "L1_conv_A_logs": _L1_conv_in["A_logs"],
        "L1_conv_Ds": _L1_conv_in["Ds"],
        "L1_conv_out_norm_g": _L1_conv_in["out_norm_g"],
        "L1_conv_out_norm_b": _L1_conv_in["out_norm_b"],
        "L1_conv_out_proj_w": _L1_conv_in["out_proj_w"],
    }

def reference(x, L0_conv_W_in, L0_conv_conv_w, L0_conv_conv_b, L0_conv_x_proj_weight, L0_conv_A_logs, L0_conv_Ds, L0_conv_dt_bias, L0_conv_init_states, L0_conv_W_out, L0_conv_W1, L0_conv_b1, L0_conv_W2, L0_conv_b2, L1_conv_bn1_g, L1_conv_bn1_b, L1_conv_bn1_m, L1_conv_bn1_v, L1_conv_bn2_g, L1_conv_bn2_b, L1_conv_bn2_m, L1_conv_bn2_v, L1_conv_bn3_g, L1_conv_bn3_b, L1_conv_bn3_m, L1_conv_bn3_v, L1_conv_conv1_w, L1_conv_conv1_b, L1_conv_conv2_w, L1_conv_conv2_b, L1_conv_conv3_w, L1_conv_conv3_b, L1_conv_ln_g, L1_conv_ln_b, L1_conv_in_proj_w, L1_conv_conv2d_w, L1_conv_conv2d_b, L1_conv_x_proj_w, L1_conv_dt_proj_w, L1_conv_dt_proj_b, L1_conv_A_logs, L1_conv_Ds, L1_conv_out_norm_g, L1_conv_out_norm_b, L1_conv_out_proj_w):
    import jax
    import jax.numpy as jnp
    def _L0_conv_ref(x, W_in, conv_w, conv_b, x_proj_weight, A_logs, Ds, dt_bias, init_states, W_out, W1, b1, W2, b2):
        import jax, jax.numpy as jnp
        import numpy as np
        import math
        B, H, W, CIN = (8, 64, 64, 192)
        INNER, K, N, P = (384, 2, 32, 64)
        NHK = INNER // P
        NH = K * NHK
        HID = 4 * CIN

        def _silu(v):
            return v * jax.nn.sigmoid(v)
        Bb, Hh, Ww, Cin = x.shape
        L = Hh * Ww
        inner = W_in.shape[0] // 2
        shortcut = x
        xz = jnp.einsum('bhwc,dc->bhwd', x, W_in)
        xl, z = jnp.split(xz, 2, axis=-1)
        xc = jnp.transpose(xl, (0, 3, 1, 2))
        xc = jax.lax.conv_general_dilated(xc, conv_w, (1, 1), 'SAME', feature_group_count=inner, dimension_numbers=('NCHW', 'OIHW', 'NCHW'))
        xc = _silu(xc + conv_b[None, :, None, None])
        xs = jnp.stack([xc.reshape(Bb, inner, L), jnp.transpose(xc, (0, 1, 3, 2)).reshape(Bb, inner, L)], axis=1)
        BCdt = jnp.einsum('bkdl,kcd->blkc', xs, x_proj_weight)
        Bs = BCdt[..., :N]
        Cs = BCdt[..., N:2 * N]
        dt = BCdt[..., 2 * N:].reshape(Bb, L, NH)
        xh = jnp.transpose(xs, (0, 3, 1, 2)).reshape(Bb, L, NH, P)
        dt = jax.nn.softplus(dt + dt_bias)
        A = -jnp.exp(A_logs)
        da = jnp.exp(dt * A)
        dtx = dt[..., None] * xh
        Bh = jnp.repeat(Bs, NHK, axis=2)
        Ch = jnp.repeat(Cs, NHK, axis=2)
        h0 = jnp.broadcast_to(init_states, (Bb,) + init_states.shape)

        def step(h, inp):
            da_t, dtx_t, B_t, C_t = inp
            h = da_t[..., None, None] * h + dtx_t[..., None] * B_t[:, :, None, :]
            y_t = jnp.einsum('bhpn,bhn->bhp', h, C_t)
            return (h, y_t)
        _, ys = jax.lax.scan(step, h0, (jnp.moveaxis(da, 1, 0), jnp.moveaxis(dtx, 1, 0), jnp.moveaxis(Bh, 1, 0), jnp.moveaxis(Ch, 1, 0)))
        y = jnp.moveaxis(ys, 0, 1) + Ds[None, None, :, None] * xh
        out_y = jnp.transpose(y.reshape(Bb, L, K, inner), (0, 2, 3, 1))
        y0 = out_y[:, 0].reshape(Bb, inner, Hh, Ww)
        y1 = jnp.transpose(out_y[:, 1].reshape(Bb, inner, Ww, Hh), (0, 1, 3, 2))
        yr = jnp.transpose((y0 + y1).reshape(Bb, inner, L), (0, 2, 1)).reshape(Bb, Hh, Ww, inner)
        yg = yr * _silu(z)
        out = shortcut + jnp.einsum('bhwd,cd->bhwc', yg, W_out)
        h1 = _silu(jnp.einsum('...c,dc->...d', out, W1) + b1)
        mlp = jnp.einsum('...d,cd->...c', h1, W2) + b2
        return out + mlp

    def _L1_conv_ref(x, bn1_g, bn1_b, bn1_m, bn1_v, bn2_g, bn2_b, bn2_m, bn2_v, bn3_g, bn3_b, bn3_m, bn3_v, conv1_w, conv1_b, conv2_w, conv2_b, conv3_w, conv3_b, ln_g, ln_b, in_proj_w, conv2d_w, conv2d_b, x_proj_w, dt_proj_w, dt_proj_b, A_logs, Ds, out_norm_g, out_norm_b, out_proj_w):
        import jax, jax.numpy as jnp
        import numpy as np
        from jax import lax
        EPS = 1e-05
        Bq, Hq, Wq, Cq = (8, 56, 56, 192)
        D_HALF, D_INNER, D_STATE, DT_RANK, K = (96, 192, 16, 6, 4)

        def _bn(x, g, b, m, v):
            return (x - m) * (g * lax.rsqrt(v + EPS)) + b

        def _ln(x, g, b):
            mu = jnp.mean(x, -1, keepdims=True)
            var = jnp.mean((x - mu) ** 2, -1, keepdims=True)
            return (x - mu) * lax.rsqrt(var + EPS) * g + b

        def _conv(x, w, b, groups=1):
            y = lax.conv_general_dilated(x, w, (1, 1), 'SAME', dimension_numbers=('NHWC', 'HWIO', 'NHWC'), feature_group_count=groups)
            return y + b

        def _forward(x, bn1_g, bn1_b, bn1_m, bn1_v, bn2_g, bn2_b, bn2_m, bn2_v, bn3_g, bn3_b, bn3_m, bn3_v, conv1_w, conv1_b, conv2_w, conv2_b, conv3_w, conv3_b, ln_g, ln_b, in_proj_w, conv2d_w, conv2d_b, x_proj_w, dt_proj_w, dt_proj_b, A_logs, Ds, out_norm_g, out_norm_b, out_proj_w):
            B, H, W, C = x.shape
            L = H * W
            xl, xr = (x[..., :D_HALF], x[..., D_HALF:])
            y = _bn(xl, bn1_g, bn1_b, bn1_m, bn1_v)
            y = _conv(y, conv1_w, conv1_b)
            y = jax.nn.relu(_bn(y, bn2_g, bn2_b, bn2_m, bn2_v))
            y = _conv(y, conv2_w, conv2_b)
            y = jax.nn.relu(_bn(y, bn3_g, bn3_b, bn3_m, bn3_v))
            xl_out = jax.nn.relu(_conv(y, conv3_w, conv3_b))
            xr_n = _ln(xr, ln_g, ln_b)
            xz = jnp.einsum('bhwc,ec->bhwe', xr_n, in_proj_w)
            xi, z = (xz[..., :D_INNER], xz[..., D_INNER:])
            xi = jax.nn.silu(_conv(xi, conv2d_w, conv2d_b, groups=D_INNER))
            xc = jnp.transpose(xi, (0, 3, 1, 2))
            x_hw = xc.reshape(B, D_INNER, L)
            x_wh = jnp.transpose(xc, (0, 1, 3, 2)).reshape(B, D_INNER, L)
            x2 = jnp.stack([x_hw, x_wh], 1)
            xs4 = jnp.concatenate([x2, jnp.flip(x2, -1)], 1)
            x_dbl = jnp.einsum('bkdl,kcd->bkcl', xs4, x_proj_w)
            dts = x_dbl[:, :, :DT_RANK]
            Bs = x_dbl[:, :, DT_RANK:DT_RANK + D_STATE]
            Cs = x_dbl[:, :, DT_RANK + D_STATE:]
            delta = jax.nn.softplus(jnp.einsum('bkrl,kdr->bkdl', dts, dt_proj_w) + dt_proj_b[None, :, :, None])
            A = -jnp.exp(A_logs)

            def step(h, t):
                u_t, d_t, b_t, c_t = t
                h = jnp.exp(d_t[..., None] * A) * h + (d_t * u_t)[..., None] * b_t[:, :, None, :]
                return (h, jnp.einsum('bkdn,bkn->bkd', h, c_t))
            scan_in = (jnp.moveaxis(xs4, -1, 0), jnp.moveaxis(delta, -1, 0), jnp.moveaxis(Bs, -1, 0), jnp.moveaxis(Cs, -1, 0))
            h0 = jnp.zeros((B, K, D_INNER, D_STATE), x.dtype)
            _, ys = lax.scan(step, h0, scan_in)
            ys = jnp.moveaxis(ys, 0, -1) + Ds[None, :, :, None] * xs4

            def wh2hw(t):
                return jnp.transpose(t.reshape(B, D_INNER, W, H), (0, 1, 3, 2)).reshape(B, D_INNER, L)
            yv = ys[:, 0] + jnp.flip(ys[:, 2], -1) + wh2hw(ys[:, 1]) + wh2hw(jnp.flip(ys[:, 3], -1))
            yv = jnp.transpose(yv, (0, 2, 1)).reshape(B, H, W, D_INNER)
            yv = _ln(yv, out_norm_g, out_norm_b) * jax.nn.silu(z)
            xr_out = jnp.einsum('bhwe,ce->bhwc', yv, out_proj_w)
            fused = jnp.concatenate([xl_out, xr_out], -1)
            fused = jnp.swapaxes(fused.reshape(B, H, W, 2, C // 2), 3, 4).reshape(B, H, W, C)
            return fused + x
        return _forward(x, bn1_g, bn1_b, bn1_m, bn1_v, bn2_g, bn2_b, bn2_m, bn2_v, bn3_g, bn3_b, bn3_m, bn3_v, conv1_w, conv1_b, conv2_w, conv2_b, conv3_w, conv3_b, ln_g, ln_b, in_proj_w, conv2d_w, conv2d_b, x_proj_w, dt_proj_w, dt_proj_b, A_logs, Ds, out_norm_g, out_norm_b, out_proj_w)

    def _gn(v, G=32, eps=1e-5):
        B_, H_, W_, C_ = v.shape
        g = v.reshape(B_, H_, W_, G, C_ // G)
        m = jnp.mean(g, axis=(1, 2, 4), keepdims=True)
        s = jnp.var(g, axis=(1, 2, 4), keepdims=True)
        return ((g - m) / jnp.sqrt(s + eps)).reshape(v.shape)

    def _ln_c(v, eps=1e-6):
        m = jnp.mean(v, axis=-1, keepdims=True)
        s = jnp.var(v, axis=-1, keepdims=True)
        return (v - m) / jnp.sqrt(s + eps)

    def _ln_t(v, eps=1e-5):
        m = jnp.mean(v, axis=-1, keepdims=True)
        s = jnp.var(v, axis=-1, keepdims=True)
        return (v - m) / jnp.sqrt(s + eps)

    def _to_tokens(v):
        B_, H_, W_, C_ = v.shape
        return v.reshape(B_, H_ * W_, C_)
    def _from_tokens(t, like):
        return t.reshape(like.shape)

    x = _L0_conv_ref(x, L0_conv_W_in, L0_conv_conv_w, L0_conv_conv_b, L0_conv_x_proj_weight, L0_conv_A_logs, L0_conv_Ds, L0_conv_dt_bias, L0_conv_init_states, L0_conv_W_out, L0_conv_W1, L0_conv_b1, L0_conv_W2, L0_conv_b2)
    x = _L1_conv_ref(x, L1_conv_bn1_g, L1_conv_bn1_b, L1_conv_bn1_m, L1_conv_bn1_v, L1_conv_bn2_g, L1_conv_bn2_b, L1_conv_bn2_m, L1_conv_bn2_v, L1_conv_bn3_g, L1_conv_bn3_b, L1_conv_bn3_m, L1_conv_bn3_v, L1_conv_conv1_w, L1_conv_conv1_b, L1_conv_conv2_w, L1_conv_conv2_b, L1_conv_conv3_w, L1_conv_conv3_b, L1_conv_ln_g, L1_conv_ln_b, L1_conv_in_proj_w, L1_conv_conv2d_w, L1_conv_conv2d_b, L1_conv_x_proj_w, L1_conv_dt_proj_w, L1_conv_dt_proj_b, L1_conv_A_logs, L1_conv_Ds, L1_conv_out_norm_g, L1_conv_out_norm_b, L1_conv_out_proj_w)
    return x


_drawn_inputs = setup_inputs


def setup_inputs(seed=0):
    import zlib

    import numpy as np

    out = dict(_drawn_inputs(seed))
    spreads = {'L0_conv_conv_b': (0.0, 0.1),
     'L0_conv_Ds': (1.0, 0.2),
     'L0_conv_init_states': (0.0, 0.1),
     'L0_conv_b1': (0.0, 0.1),
     'L0_conv_b2': (0.0, 0.1),
     'L1_conv_bn1_g': (1.0, 0.2),
     'L1_conv_bn1_b': (0.0, 0.1),
     'L1_conv_bn2_g': (1.0, 0.2),
     'L1_conv_bn2_b': (0.0, 0.1),
     'L1_conv_bn3_g': (1.0, 0.2),
     'L1_conv_bn3_b': (0.0, 0.1),
     'L1_conv_ln_g': (1.0, 0.2),
     'L1_conv_ln_b': (0.0, 0.1),
     'L1_conv_Ds': (1.0, 0.2),
     'L1_conv_out_norm_g': (1.0, 0.2),
     'L1_conv_out_norm_b': (0.0, 0.1)}
    factors = {}
    for name, (base, spread) in spreads.items():
        noise = np.random.default_rng([zlib.crc32(name.encode()), seed]).standard_normal(out[name].shape)
        drawn = base * np.exp(spread * noise) if base else spread * noise
        out[name] = jnp.asarray(drawn.astype(out[name].dtype))
    for name, factor in factors.items():
        out[name] = (out[name] * factor).astype(out[name].dtype)
    return out
```

```python
from contextlib import ExitStack

import numpy as np

import concourse.bass as bass
from concourse import mybir

F32 = mybir.dt.float32
BF = mybir.dt.bfloat16
ALU = mybir.AluOpType
ACT = mybir.ActivationFunctionType

L = 4096
PADW = 66
PADN = PADW * PADW
MUL, ADD, SUB, MAX = ALU.mult, ALU.add, ALU.subtract, ALU.max

VCOL = {}
_at = 0
for _name, _n in [("cb", 3), ("ds0", 6), ("b1", 6), ("b2", 2), ("alog0", 12), ("dtb0", 12),
                  ("bn1", 4), ("bn2", 4), ("bn3", 4), ("c1b", 1), ("c2b", 1), ("c3b", 1),
                  ("lng", 1), ("lnb", 1), ("cdb", 2), ("dtb1", 8), ("ds1", 8), ("ong", 2),
                  ("onb", 2), ("alog1", 96), ("w0", 27), ("w1", 18)]:
    VCOL[_name] = (_at, _at + _n)
    _at += _n
NV = _at

CCOL = {}
_at = 0
for _name, _n in [("ident", 128), ("tri", 128), ("ones", 128), ("red", 128), ("sel", 512),
                  ("neg", 128), ("one3", 32), ("perm", 768)]:
    CCOL[_name] = (_at, _at + _n)
    _at += _n
NC_ = _at


class Eng:

    def __init__(self, e, sem):
        self.e, self.sem, self.n = e, sem, 0

    def inc(self, inst):
        inst.then_inc(self.sem, 1)
        self.n += 1
        return (self.sem, self.n)


def program(nc, A, NB):
    with ExitStack() as ctx:
        _program(nc, A, NB, ctx)


def _program(nc, A, NB, ctx):
    def sb(n, s, d=F32):
        return ctx.enter_context(nc.sbuf_tensor(n, s, d))

    def ps(n, s):
        return ctx.enter_context(nc.psum_tensor(n, s, F32))

    def sem(n):
        return ctx.enter_context(nc.semaphore(n))

    PE, AC, DV, PO, SP = (Eng(e, sem(n)) for e, n in (
        (nc.tensor, "s_pe"), (nc.scalar, "s_act"), (nc.vector, "s_dve"), (nc.gpsimd, "s_pool"),
        (nc.sync, "s_sp")))
    engines = [PE, AC, DV, PO, SP]

    done = {}
    lanes, count = {}, {}

    def wait(eng, *steps):
        for key in steps:
            if key in done:
                eng.e.wait_ge(*done[key])
            else:
                assert key[-1] < 0, key

    def mark(key, token):
        done[key] = token

    def dma(key, lane, out, in_):
        if lane not in lanes:
            lanes[lane], count[lane] = sem(f"d_{lane}"), 0
        nc.sync.dma_start(out, in_).then_inc(lanes[lane], 16)
        count[lane] += 16
        done[key] = (lanes[lane], count[lane])

    def mm(out, w, x, start, stop):
        return nc.tensor.matmul(out, w, x, start=start, stop=stop, skip_group_check=True)

    def act(out, in_, f, **kw):
        return AC.inc(nc.scalar.activation(out, in_, f, **kw))

    def tt(out, a, b, op):
        return DV.inc(nc.vector.tensor_tensor(out, a, b, op))

    def stt(out, a, s_, b, op0, op1):
        return DV.inc(nc.vector.scalar_tensor_tensor(out, a, s_, b, op0, op1))

    def ptt(out, a, b, op):
        return PO.inc(nc.gpsimd.tensor_tensor(out, a, b, op))

    def hi(ap):
        return ap.bitcast(BF)[:, 1::2]

    def dram(n, s, d=F32):
        return nc.dram_tensor(n, s, d).ap()
    xTd = dram("xTd", (2, 96, L))
    xc0 = dram("xc0", (3, 128, L))
    tkd = dram("tkd", (L, 524))
    dtd = dram("dtd", (L, 12))
    y0d = dram("y0d", (2, L, 384))
    spd = dram("spd", (3, 384, 128), BF)
    x1d = dram("x1d", (2, 2, 96, L))
    xld = dram("xld", (2, 96, L))
    zd = dram("zd", (2, 2, 96, L))
    xcd = dram("xcd", (2, 2, 96, L))
    ptd = dram("ptd", (2, 4, 6, 96, 2, L))
    bcd = dram("bcd", (2, 4, 32, L))
    yd = dram("yd", (2, 4, 6, 4, 128, 256))

    RA = sb("RA", [128, 3 * PADN])
    RB = sb("RB", [128, 2 * L])
    WD = sb("WD", [6, 768])
    IPW = sb("IPW", [96, 8])
    WP = sb("WP", [96, 384])
    PERM = sb("PERM", [96, 768])
    CB = sb("CB", [128, 512])
    SELB = sb("SELB", [96, 512], BF)
    NEGB = sb("NEGB", [128, 128], BF)
    IDB = sb("IDB", [128, 128], BF)
    V = sb("V", [128, NV])
    DV0 = sb("DV0", [128, 48])
    A1 = sb("A1", [128, 96])
    M96 = sb("M96", [96, 96])
    M192 = sb("M192", [96, 96])
    ONE = sb("ONE", [128, 2])
    IDENT = CB[:, 0:128]
    TRI = CB[:, 128:256]
    ONES = CB[:, 256:384]
    RED = CB[:, 384:512].rearrange("p (g c) -> p g c", g=4)
    SEL = SELB[:, :].rearrange("p (g c) -> p g c", g=4)

    def vec(name, i=0, n=1, P=96):
        a = VCOL[name][0] + i
        return V[0:P, a:a + n]

    NA, NH, NHC, NBR, NPT = 2, 4, 3, 2, 2
    dA = sb("dA", [128, NA, 1024])
    H = sb("H", [128, NH, 1024])
    HC = sb("HC", [128, NHC, 1024])
    BR = sb("BR", [128, NBR, 2, 1024])
    PT = sb("PT", [96, NPT, 2, 1024])
    CR = sb("CR", [128, 24])
    YS = sb("YS", [128, 2, 256])
    PD = ps("PD", [128, 1024])
    PU = ps("PU", [128, 1024])
    PY = ps("PY", [128, 256])
    NP = 3
    PB = [ps(f"PB{i}", [128, 512]) for i in range(NP)]
    T0 = sb("T0", [128, 3, 512])
    T1 = sb("T1", [128, 3, 512])
    XT = sb("XT", [96, 2, 2, 512])
    XI = sb("XI", [128, 2, 4, 192])

    bank_no = [0]

    def bank():
        n = bank_no[0]
        bank_no[0] += 1
        wait(PE, ("emptied", n - NP))
        return n, PB[n % NP]

    def emptied(n, token):
        mark(("emptied", n), token)

    def phase():
        for eng in (PE, AC, DV, PO, SP):
            for e in (PE, AC, DV, PO):
                if e.n:
                    eng.e.wait_ge(e.sem, e.n)
            for n in lanes:
                if n[0] != "S" and count[n]:
                    eng.e.wait_ge(lanes[n], count[n])

    class Cutter:

        def __init__(self, t, size):
            self.t, self.size, self.at = t, size, 0

        def __call__(self, n, P=128):
            a = self.at
            self.at += n
            assert self.at <= self.size, (self.at, self.size)
            return self.t[0:P, a:a + n]

    def pipeline(n, *stages):
        for r in range(n + len(stages) - 1):
            for s_ in range(len(stages) - 1, -1, -1):
                if 0 <= r - s_ < n:
                    yield from stages[s_](r - s_)

    def setup():
        dma(("consts", 0), "c0", RA[:, 0:NC_], A["consts"])
        dma(("vecs", 0), "c1", V[:, :], A["vecs"])
        dma(("weights", 0), "c2", WP[:, :], A["wop"])
        dma(("weights", 0), "c2", WD[:, :], A["dtw"].rearrange("r k c -> r (k c)"))
        v = nc.vector

        def c(name, P=128):
            x, y = CCOL[name]
            return RA[0:P, x:y]
        wait(DV, ("consts", 0), ("vecs", 0))
        v.tensor_copy(CB[:, :], RA[:, 0:512])
        v.tensor_copy(SELB[:, :], c("sel", 96))
        v.tensor_copy(NEGB[:, :], c("neg"))
        v.tensor_copy(IDB[:, :], c("ident"))
        v.tensor_copy(PERM[:, :], c("perm", 96))
        v.memset(M96[:, :], 1.0 / 96)
        v.memset(M192[:, :], 1.0 / 192)
        v.memset(ONE[:, 0:1], 1.0)
        v.memset(ONE[:, 1:2], 1e-5)
        wait(AC, ("vecs", 0))
        a0 = VCOL["alog1"][0]
        act(A1[:, :], V[:, a0:a0 + 96], ACT.Exp)
        a0 = VCOL["alog0"][0]
        mark(("exps", 0), act(DV0[:, 0:12], V[:, a0:a0 + 12], ACT.Exp))
        wait(DV, ("exps", 0))
        v.tensor_scalar(A1[:, :], A1[:, :], -1.0, None, MUL)
        v.tensor_scalar(DV0[:, 0:12], DV0[:, 0:12], -1.0, None, MUL)
        d0 = VCOL["ds0"][0]
        v.tensor_tensor(DV0[:, 12:15], V[:, d0:d0 + 3], V[:, d0 + 3:d0 + 6], ADD)
        c0 = VCOL["cb"][0]
        v.tensor_scalar(DV0[:, 15:18], V[:, c0:c0 + 3], 0.5, None, MUL)
        c0 = VCOL["b1"][0]
        v.tensor_scalar(DV0[:, 18:24], V[:, c0:c0 + 6], 0.5, None, MUL)
        c0 = VCOL["cdb"][0]
        v.tensor_scalar(DV0[0:96, 24:26], V[0:96, c0:c0 + 2], 0.5, None, MUL)
        c0 = VCOL["ds1"][0]
        mark(("ds", 0), tt(DV0[0:96, 26:30], V[0:96, c0:c0 + 4], V[0:96, c0 + 4:c0 + 8], ADD))
        wait(DV, ("ds", 0))
        v.tensor_tensor(DV0[0:96, 30:32], DV0[0:96, 26:28], DV0[0:96, 28:30], ADD)
        for i in range(3):
            q = VCOL[f"bn{i + 1}"][0] + 3
            mark(("v+eps", 0), DV.inc(v.tensor_scalar(DV0[0:96, 38 + i:39 + i], V[0:96, q:q + 1], 1e-5, None, ADD)))
        wait(AC, ("v+eps", 0))
        mark(("sqrt", 0), act(DV0[0:96, 41:44], DV0[0:96, 38:41], ACT.Sqrt))
        wait(DV, ("sqrt", 0))
        mark(("rsqrt", 0), DV.inc(v.reciprocal(DV0[0:96, 38:41], DV0[0:96, 41:44])))
        wait(DV, ("rsqrt", 0))
        for i in range(3):
            tt(DV0[0:96, 32 + i:33 + i], DV0[0:96, 38 + i:39 + i], vec(f"bn{i + 1}", 0), MUL)
        v.tensor_scalar(DV0[0:96, 44:45], vec("bn1", 2), -1.0, None, MUL)
        for i in (1, 2):
            mark(("b-m", 0), tt(DV0[0:96, 44 + i:45 + i], vec(f"c{i}b"), vec(f"bn{i + 1}", 2), SUB))
        wait(DV, ("b-m", 0))
        for i in range(3):
            stt(DV0[0:96, 35 + i:36 + i], DV0[0:96, 44 + i:45 + i], DV0[0:96, 32 + i:33 + i],
                vec(f"bn{i + 1}", 1), MUL, ADD)

    def borders(img, n, P):
        for y in (0, PADW - 1):
            nc.vector.memset(img[0:P, 0:n, y, :], 0.0)
        for x in (0, PADW - 1):
            t = DV.inc(nc.vector.memset(img[0:P, 0:n, 1:PADW - 1, x], 0.0))
        return t

    def conv9(o, P, wt, img, i):
        for tap in range(9):
            dy, dx = divmod(tap, 3)
            t = mm(o[0:P, :], wt(tap), img[:, 8 * i + dy:8 * i + dy + 8, dx:dx + 64], tap == 0, tap == 8)
        return PE.inc(t)

    def layer0(b, par):
        phase()
        ra, rb = Cutter(RA, 3 * PADN), Cutter(RB, 2 * L)
        XP = ra(3 * PADN).rearrange("p (j y x) -> p j y x", j=3, y=PADW)
        wx = rb(768, 96).rearrange("p (k c) -> p k c", k=2)
        DG = rb(27 * 128).rearrange("p (t c) -> p t c", t=27)
        wxp = rb(420).rearrange("p (j c) -> p j c", j=3)
        XJ = [rb(512) for _ in range(3)]
        TK = [rb(524) for _ in range(2)]
        PRK = rb(384)
        dma(("a.wx", 0), "w0", wx, A["win"][:, :, 0:384])
        dma(("a.wxp", 0), "w1", wxp, A["wxp0"])
        w0 = VCOL["w0"][0]
        for i in range(27):
            mark(("a.diag", 0), PO.inc(nc.gpsimd.tensor_scalar(DG[:, i, :], IDENT, V[:, w0 + i:w0 + i + 1], 1.0, MUL, MUL)))
        mark(("a.rim", 0), borders(XP, 3, 128))
        yield 2
        xv = A["x"][b].rearrange("(i q p) c -> i p q c", q=4, p=128)

        def load(i):
            wait(SP, ("a.xT", 2 * (i - 2) + 1))
            dma(("a.x", i), f"xi{i % 2}", XI[:, i % 2, :, :], xv[i])
            yield 0

        def turn(i):
            wait(PE, ("a.x", i))
            for hh in range(2):
                n, pb = bank()
                for q in range(4):
                    t = nc.tensor.transpose(pb[0:96, q * 128:(q + 1) * 128],
                                            XI[:, i % 2, q, hh * 96:(hh + 1) * 96], IDENT)
                mark(("a.xT", 2 * i + hh), PE.inc(t))
                wait(AC, ("a.xT", 2 * i + hh), ("a.proj", i - 2), ("a.xTout", i - 2))
                emptied(n, act(XT[:, i % 2, hh, :], pb[0:96, :], ACT.Copy))
            mark(("a.xTc", i), done["emptied", n])
            yield 1
            wait(SP, ("a.xTc", i))
            dma(("a.xTout", i), f"xt{i % 2}", xTd[:, :, i * 512:(i + 1) * 512].rearrange("k p n -> p k n"),
                XT[:, i % 2, :, :])

        def project(i):
            wait(PE, ("a.wx", 0), ("a.xTc", i))
            for j in range(3):
                n, pb = bank()
                for k in range(2):
                    t = mm(pb[:, :], wx[:, k, j * 128:(j + 1) * 128], XT[:, i % 2, k, :], k == 0, k == 1)
                mark(("a.proj", i), PE.inc(t))
                wait(AC, ("a.proj", i))
                emptied(n, act(XP[:, j, 1 + 8 * i:9 + 8 * i, 1:65], pb[:, :].rearrange("p (y x) -> p y x", y=8),
                               ACT.Copy))
                yield 1.7
            mark(("a.rows", i), done["emptied", n])
        yield from pipeline(8, load, turn, project)

        tkv = tkd.rearrange("(i p) c -> i p c", p=128)
        wait(PE, ("a.diag", 0), ("a.rim", 0))

        def conv(m):
            i, j = divmod(m, 3)
            wait(PE, ("a.rows", min(i + 1, 7)))
            n, pb = bank()
            mark(("a.conv", m), conv9(pb, 128, lambda tap: DG[:, j * 9 + tap, :], XP[:, j], i))
            yield 7.7
            wait(AC, ("a.conv", m), ("a.silu", m - 3))
            act(T0[:, m % 3, :], pb[:, :], ACT.Tanh, bias=DV0[:, 15 + j:16 + j], scale=0.5)
            emptied(n, act(T1[:, m % 3, :], pb[:, :], ACT.Identity, bias=DV0[:, 15 + j:16 + j], scale=0.5))
            wait(DV, ("emptied", n), ("a.tproj", 4 * (i - 1) + 3), ("a.xcout", m - 3))
            mark(("a.silu", m), stt(XJ[j], T0[:, m % 3, :], 1.0, T1[:, m % 3, :], ADD, MUL))
            yield 0
            wait(SP, ("a.silu", m))
            dma(("a.xcout", m), f"xj{j}", xc0[j, :, i * 512:(i + 1) * 512], XJ[j])
            if j < 2:
                return
            for q in range(4):
                c = 4 * i + q
                qs = slice(q * 128, (q + 1) * 128)
                wait(PE, ("a.silu", m))
                n, pb = bank()
                for j_ in range(3):
                    t = nc.tensor.transpose(pb[:, j_ * 128:(j_ + 1) * 128], XJ[j_][:, qs], IDENT)
                mark(("a.tturn", c), PE.inc(t))
                n2, pb2 = bank()
                for j_ in range(3):
                    t = mm(pb2[:, 0:140], XJ[j_][:, qs], wxp[:, j_, :], j_ == 0, j_ == 2)
                mark(("a.tproj", c), PE.inc(t))
                tk = TK[c % 2]
                wait(AC, ("a.tproj", c), ("a.tkout", c - 2))
                emptied(n, act(tk[:, 70:454], pb[:, 0:384], ACT.Copy))
                act(tk[:, 0:70], pb2[:, 0:70], ACT.Copy)
                act(tk[:, 454:524], pb2[:, 70:140], ACT.Copy)
                emptied(n2, act(PRK[:, c * 12:c * 12 + 12].rearrange("p (k h) -> p k h", k=2),
                                pb2[:, 0:140].rearrange("p (k c) -> p k c", k=2)[:, :, 64:70], ACT.Copy))
                yield 1.8
                wait(SP, ("emptied", n2))
                dma(("a.tkout", c), f"tk{c % 2}", tkv[c], tk)
        wait(PE, ("a.wxp", 0))
        yield from pipeline(24, conv)

        a = VCOL["dtb0"][0]
        wait(DV, ("emptied", bank_no[0] - 1))
        tt(PRK.rearrange("p (c h) -> p c h", c=32), PRK.rearrange("p (c h) -> p c h", c=32),
           V[:, a:a + 12].unsqueeze(1).to_broadcast([128, 32, 12]), ADD)
        phase()
        ra = Cutter(RA, 3 * PADN)
        S0, S1, S2, DT, AT, ES = (ra(384) for _ in range(6))
        DTT = ra(768).rearrange("p (u w h) -> p u w h", u=64, w=2)
        SB_ = ra(576).bitcast(BF).rearrange("p (a n) -> p a n", a=3)
        HS = ra(768, 32)
        rb2 = Cutter(RB, 2 * L)
        RL = [rb2(1536, 96).bitcast(BF).rearrange("p (a n) -> p a n", a=2) for _ in range(2)]
        for rl in RL:
            mark(("b.zero", 0), DV.inc(nc.vector.memset(rl, 0.0)))
        wait(DV, ("b.zero", 0))
        for rl in RL:
            nc.vector.memset(rl[32:64, 0, :], -1.0)
            mark(("b.rows", 0), DV.inc(nc.vector.memset(rl[0:32, 1, :], 1.0)))
        mark(("b.abs", 0), act(S1, PRK, ACT.Abs))
        wait(AC, ("b.abs", 0))
        mark(("b.exp", 0), act(S1, S1, ACT.Exp, scale=-1.0))
        wait(AC, ("b.exp", 0))
        mark(("b.ln", 0), act(S1, S1, ACT.Ln, bias=ONE[:, 0:1]))
        wait(DV, ("b.ln", 0))
        mark(("b.steps", 0), stt(S0, PRK, 0.0, S1, MAX, ADD))
        wait(SP, ("b.steps", 0))
        dma(("b.dtout", 0), "w0", dtd.rearrange("(c p) h -> p c h", p=128), S0.rearrange("p (c h) -> p c h", c=32))
        dtv = DT.rearrange("p (c k h) -> p c k h", c=32, k=2)
        wait(DV, ("b.steps", 0))
        mark(("b.dt0", 0), DV.inc(nc.vector.tensor_copy(
            dtv[:, :, 0, :], S0.rearrange("p (c k h) -> p c k h", c=32, k=2)[:, :, 0, :])))
        dcol = dtd.rearrange("(h c w) n -> w h c n", h=64, w=2)
        wait(SP, ("b.dtout", 0))
        for w in range(2):
            dma(("b.dt1", 0), "w1", dtv[64 * w:64 * w + 64, :, 1, :], dcol[w][:, :, 6:12])
        yield 3
        wait(DV, ("b.dt0", 0), ("b.dt1", 0), ("b.dtout", 0))
        mark(("b.la", 0), tt(S0.rearrange("p (c h) -> p c h", c=32), DT.rearrange("p (c h) -> p c h", c=32),
                             DV0[:, 0:12].unsqueeze(1).to_broadcast([128, 32, 12]), MUL))
        (n1, p1), (n2, p2) = bank(), bank()
        wait(PE, ("b.la", 0))
        mm(p1[:, 0:384], TRI, S0, True, True)
        mark(("b.sums", 0), PE.inc(mm(p2[:, 0:384], ONES, S0, True, True)))
        wait(DV, ("b.sums", 0))
        mark(("b.cum", 0), DV.inc(nc.vector.tensor_copy(S1, p1[:, 0:384])))
        emptied(n1, done["b.cum", 0])
        wait(DV, ("b.cum", 0))
        mark(("b.left", 0), tt(S2, p2[:, 0:384], S1, SUB))
        wait(AC, ("b.left", 0))
        emptied(n2, act(AT, p2[:, 0:384], ACT.Exp))
        mark(("b.w", 0), act(S2, S2, ACT.Exp))
        mark(("b.es", 0), act(ES, S1, ACT.Exp))
        yield 2
        d3 = DT.rearrange("p (u h) -> p u h", u=64)
        mark(("b.dtt0", 0), DV.inc(nc.vector.tensor_copy(DTT[:, :, 0, :], d3)))
        wait(DV, ("b.w", 0))
        mark(("b.dtt", 0), tt(DTT[:, :, 1, :], d3, S2.rearrange("p (u h) -> p u h", u=64), MUL))
        n, pb = bank()
        wait(PE, ("b.cum", 0))
        for j in range(3):
            t = nc.tensor.transpose(pb[:, j * 128:(j + 1) * 128], S1[:, j * 128:(j + 1) * 128], IDENT)
        mark(("b.rowT", 0), PE.inc(t))
        wait(DV, ("b.rowT", 0))
        mark(("b.part0", 0), DV.inc(nc.vector.tensor_copy(SB_[:, 0, :], pb[:, 0:384])))
        wait(DV, ("b.part0", 0))
        mark(("b.rest1", 0), tt(S0, pb[:, 0:384], SB_[:, 0, :], SUB))
        emptied(n, done["b.rest1", 0])
        wait(DV, ("b.rest1", 0))
        mark(("b.part1", 0), DV.inc(nc.vector.tensor_copy(SB_[:, 1, :], S0)))
        wait(DV, ("b.part1", 0))
        mark(("b.parts", 0), tt(SB_[:, 2, :], S0, SB_[:, 1, :], SUB))
        wait(SP, ("b.parts", 0))
        for i in range(3):
            dma(("b.spout", 0), "w2", spd[i].rearrange("(j q) t -> q j t", q=128),
                SB_[:, i, :].rearrange("p (j t) -> p j t", j=3))
        dma(("b.state", -1), "w3", HS, A["h0"])
        done["b.state0", -1] = done["b.state1", -1] = done["b.state", -1]
        yield 3
        TK = [ra(454) for _ in range(4)]
        CC = [ra(256, 32) for _ in range(2)]
        DX = [ra(768) for _ in range(2)]
        EE = [ra(768) for _ in range(2)]
        MM = [rb2(768) for _ in range(2)]
        YO = [ra(384) for _ in range(4)]
        tkc = tkd.rearrange("(h c w) n -> c w h n", h=64, w=2)
        ycol = y0d[1].rearrange("(h c w) n -> c w h n", h=64, w=2)
        wait(PE, ("b.rows", 0))

        def fetch(u):
            c, k = divmod(u, 2)
            if k == 0:
                wait(SP, ("b.decay", u - 3), ("b.spout", 0))
                src = spd[:, c * 12:c * 12 + 12, :].rearrange("a h t -> a (h t)")
                dma(("b.rl", c), f"rl{c % 2}", RL[c % 2][0:3, 0, :], src)
                dma(("b.rl", c), f"rl{c % 2}", RL[c % 2][32:35, 1, :], src)
            wait(SP, ("b.upd", u - 4), ("b.dx", u - 4))
            tk = TK[u % 4]
            if k == 0:
                dma(("b.tk", u), f"tk{u % 4}", tk, tkd[c * 128:(c + 1) * 128, 0:454])
            else:
                dma(("b.tk", u), f"tk{u % 4}", tk, tkc[c][:, :, 70:524])
            yield 0

        def mix(u):
            c, k = divmod(u, 2)
            tk, xo, po = TK[u % 4], (70, 0)[k], (0, 384)[k]
            cc, dx, ee, mx = CC[u % 2], DX[u % 2], EE[u % 2], MM[u % 2]
            wait(PE, ("b.tk", u))
            n, pb = bank()
            nc.tensor.transpose(pb[0:32, 0:128], tk[:, po:po + 32], IDENT)
            mark(("b.cbT", u), PE.inc(nc.tensor.transpose(pb[0:32, 128:256], tk[:, po + 32:po + 64], IDENT)))
            wait(AC, ("b.cbT", u), ("b.carry", u - 2))
            mark(("b.cb", u), act(cc, pb[0:32, 0:256], ACT.Copy))
            emptied(n, done["b.cb", u])
            wait(DV, ("b.tk", u), ("b.dtt0", 0), ("b.dtt", 0), ("b.upd", u - 2))
            mark(("b.dx", u), tt(
                dx.rearrange("p (w h q) -> p w h q", w=2, h=6),
                tk[:, xo:xo + 384].rearrange("p (h q) -> p h q", h=6).unsqueeze(1).to_broadcast([128, 2, 6, 64]),
                DTT[:, u, :, :].unsqueeze(3).to_broadcast([128, 2, 6, 64]), MUL))
            wait(PE, ("b.rl", c))
            for hf in range(2):
                n, pb = bank()
                for h in range(3):
                    q = (k * 6 + hf * 3 + h) * 128
                    mm(pb[:, h * 128:(h + 1) * 128], RL[c % 2][:, 1, q:q + 128], RL[c % 2][:, 0, q:q + 128],
                       h == 0, False)
                t = mm(pb[:, 0:384].rearrange("p (h t) -> p h t", h=3), IDB[:, :],
                       NEGB[:, :].unsqueeze(1).to_broadcast([128, 3, 128]), False, True)
                mark(("b.decay", u), PE.inc(t))
                wait(AC, ("b.decay", u), ("b.mix", u - 2))
                emptied(n, act(ee[:, hf * 384:(hf + 1) * 384], pb[:, 0:384], ACT.Exp))
                yield 0.7
            mark(("b.exp", u), done["emptied", n])
            n, pb = bank()
            wait(PE, ("b.cb", u))
            mark(("b.g", u), PE.inc(mm(pb[:, 0:128], cc[:, 128:256], cc[:, 0:128], True, True)))
            wait(DV, ("b.exp", u), ("b.g", u), ("b.y", u - 2))
            mark(("b.mix", u), tt(mx.rearrange("p (h t) -> p h t", h=6), ee.rearrange("p (h t) -> p h t", h=6),
                                  pb[:, 0:128].unsqueeze(1).to_broadcast([128, 6, 128]), MUL))
            emptied(n, done["b.mix", u])
            yield 0.5

        def out(u):
            c, k = divmod(u, 2)
            tk, xo, po = TK[u % 4], (70, 0)[k], (0, 384)[k]
            cc, dx, mx, yo = CC[u % 2], DX[u % 2], MM[u % 2], YO[u % 4]
            hv = HS[:, k * 384:(k + 1) * 384]
            n, pc = bank()
            wait(PE, ("b.cb", u), (f"b.state{k}", u - 2) if u > 1 else ("b.state", -1))
            mark(("b.carry", u), PE.inc(mm(pc[:, 0:384], cc[:, 0:128], hv, True, True)))
            wait(DV, ("b.carry", u), ("b.es", 0))
            mark(("b.fade", u), tt(
                hv.rearrange("p (h q) -> p h q", h=6), hv.rearrange("p (h q) -> p h q", h=6),
                AT[0:32, u * 6:u * 6 + 6].unsqueeze(2).to_broadcast([32, 6, 64]), MUL))
            wait(DV, ("b.yout", u - 4))
            mark(("b.ycarry", u), tt(
                yo.rearrange("p (h q) -> p h q", h=6), pc[:, 0:384].rearrange("p (h q) -> p h q", h=6),
                ES[:, u * 6:u * 6 + 6].unsqueeze(2).to_broadcast([128, 6, 64]), MUL))
            emptied(n, done["b.ycarry", u])
            n, pst = bank()
            wait(PE, ("b.dx", u))
            mark(("b.upd", u), PE.inc(mm(pst[0:32, 0:384], tk[:, po + 32:po + 64], dx[:, 384:768], True, True)))
            wait(DV, ("b.upd", u), ("b.fade", u))
            mark((f"b.state{k}", u), tt(hv, hv, pst[0:32, 0:384], ADD))
            emptied(n, done[f"b.state{k}", u])
            yield 1.2
            n, py = bank()
            wait(PE, ("b.mix", u))
            for h in range(6):
                t = mm(py[:, h * 64:(h + 1) * 64], mx[:, h * 128:(h + 1) * 128], dx[:, h * 64:(h + 1) * 64], True, True)
            mark(("b.y", u), PE.inc(t))
            wait(DV, ("b.y", u), ("b.ycarry", u))
            mark(("b.ysum", u), tt(yo, yo, py[:, 0:384], ADD))
            emptied(n, done["b.ysum", u])
            yield 0.8

        def store(u):
            c, k = divmod(u, 2)
            wait(SP, ("b.ysum", u))
            if k == 0:
                dma(("b.yout", u), f"yo{u % 4}", y0d[0, c * 128:(c + 1) * 128, :], YO[u % 4])
            else:
                dma(("b.yout", u), f"yo{u % 4}", ycol[c], YO[u % 4])
            yield 0
        yield from pipeline(64, fetch, lambda u: iter(()), mix, out, store)

        phase()
        ra, rb = Cutter(RA, 3 * PADN), Cutter(RB, 2 * L)
        HB = [ra(512) for _ in range(6)]
        YG = [ra(512) for _ in range(3)]
        XO, XS = [ra(1024, 96) for _ in range(2)], [ra(1024, 96) for _ in range(2)]
        Y0, Y1 = ra(1536), ra(1536)
        wz = rb(768, 96).rearrange("p (k c) -> p k c", k=2)
        wo = rb(576).rearrange("p (j c) -> p j c", j=3)
        w1 = rb(1536, 96).rearrange("p (k c) -> p k c", k=2)
        w2 = rb(1152).rearrange("p (j c) -> p j c", j=6)
        XCR = [rb(1536) for _ in range(2)]
        dma(("c.w", 0), "w0", wz, A["win"][:, :, 384:768])
        dma(("c.w", 0), "w0", wo, A["wout0"])
        dma(("c.w", 0), "w0", w1, A["w1"])
        dma(("c.w", 0), "w0", w2, A["w2"])
        yv = y0d.rearrange("k (i q p) c -> k i p q c", q=4, p=128)

        def cload(i):
            cs_ = slice(i * 512, (i + 1) * 512)
            wait(SP, ("c.xo", i - 2), ("c.yT", 3 * (i - 1) + 2), ("c.ysum", i - 1), ("c.yr", 3 * (i - 2) + 2))
            dma(("c.y0", i), "y0", Y0.rearrange("p (q c) -> p q c", q=4), yv[0, i])
            dma(("c.y1", i), "y1", Y1.rearrange("p (q c) -> p q c", q=4), yv[1, i])
            dma(("c.xT", i), f"xt{i % 2}", XT[:, i % 2, :, :], xTd[:, :, cs_].rearrange("k p n -> p k n"))
            dma(("c.xc", i), f"xc{i % 2}", XCR[i % 2].rearrange("p (j n) -> p j n", j=3),
                xc0[:, :, cs_].rearrange("j p n -> p j n"))
            yield 0

        def gate(i):
            wait(PO, ("c.y0", i), ("c.y1", i))
            mark(("c.ysum", i), ptt(Y0, Y0, Y1, ADD))
            wait(PE, ("c.xT", i), ("c.w", 0))
            for j in range(3):
                m = 3 * i + j
                n, pb = bank()
                for k in range(2):
                    t = mm(pb[:, :], wz[:, k, j * 128:(j + 1) * 128], XT[:, i % 2, k, :], k == 0, k == 1)
                mark(("c.z", m), PE.inc(t))
                wait(AC, ("c.z", m), ("c.yg", m - 3))
                mark(("c.tanh", m), act(T0[:, m % 3, :], pb[:, :], ACT.Tanh, scale=0.5))
                wait(DV, ("c.tanh", m))
                mark(("c.silu", m), stt(T0[:, m % 3, :], T0[:, m % 3, :], 1.0, pb[:, :], ADD, MUL))
                emptied(n, done["c.silu", m])
                yield 1.7
                n, pb = bank()
                wait(PE, ("c.ysum", i))
                for q in range(4):
                    t = nc.tensor.transpose(pb[:, q * 128:(q + 1) * 128],
                                            Y0[:, q * 384 + j * 128:q * 384 + (j + 1) * 128], IDENT)
                mark(("c.yT", m), PE.inc(t))
                wait(DV, ("c.yT", m), ("c.xc", i))
                mark(("c.yr", m), stt(T1[:, m % 3, :], XCR[i % 2][:, j * 512:(j + 1) * 512], DV0[:, 12 + j:13 + j],
                                      pb[:, :], MUL, ADD))
                emptied(n, done["c.yr", m])
                wait(DV, ("c.silu", m), ("c.yr", m), ("c.out", i - 1))
                mark(("c.yg", m), stt(YG[j], T0[:, m % 3, :], 0.5, T1[:, m % 3, :], MUL, MUL))
                yield 0.5

        def outp(i):
            xo = XO[i % 2]
            wait(PE, ("c.yg", 3 * i + 2))
            for m in range(2):
                n, pb = bank()
                for j in range(3):
                    t = mm(pb[0:96, :], wo[:, j, m * 96:(m + 1) * 96], YG[j], j == 0, j == 2)
                mark(("c.out", i), PE.inc(t))
                wait(DV, ("c.out", i), ("c.x1", i - 2), ("c.xT", i))
                mark(("c.xo", i), tt(xo[:, m * 512:(m + 1) * 512], pb[0:96, :], XT[:, i % 2, m, :], ADD))
                emptied(n, done["c.xo", i])
                yield 2.6

        def mlp(i):
            xo, xs = XO[i % 2], XS[i % 2]
            cs_ = slice(i * 512, (i + 1) * 512)
            wait(PE, ("c.xo", i))
            for j in range(6):
                m = 6 * i + j
                n, pb = bank()
                for k in range(2):
                    t = mm(pb[:, :], w1[:, k, j * 128:(j + 1) * 128], xo[:, k * 512:(k + 1) * 512], k == 0, k == 1)
                mark(("c.h", m), PE.inc(t))
                ta, tb = MA[m % 2], MB[m % 2]
                wait(AC, ("c.h", m), ("c.hs", m - 2))
                act(ta, pb[:, :], ACT.Tanh, bias=DV0[:, 18 + j:19 + j], scale=0.5)
                emptied(n, act(tb, pb[:, :], ACT.Identity, bias=DV0[:, 18 + j:19 + j], scale=0.5))
                wait(DV, ("emptied", n), ("c.mlp", i - 1))
                mark(("c.hs", m), stt(HB[j], ta, 1.0, tb, ADD, MUL))
                yield 1.7
            wait(PE, ("c.hs", 6 * i + 5))
            for m in range(2):
                n, pb = bank()
                for j in range(6):
                    t = mm(pb[0:96, :], w2[:, j, m * 96:(m + 1) * 96], HB[j], j == 0, j == 5)
                mark(("c.mlp", i), PE.inc(t))
                wait(DV, ("c.mlp", i), ("c.x1out", i - 2))
                mark(("c.x1", i), stt(xs[:, m * 512:(m + 1) * 512], pb[0:96, :], vec("b2", m),
                                      xo[:, m * 512:(m + 1) * 512], ADD, ADD))
                emptied(n, done["c.x1", i])
                yield 5.1
            wait(SP, ("c.x1", i))
            dma(("c.x1out", i), f"xs{i % 2}", x1d[par, :, :, cs_].rearrange("k p n -> p k n"),
                xs.rearrange("p (k n) -> p k n", k=2))
        MA, MB = [XI[:, i, :, :].rearrange("p a c -> p (a c)")[:, 0:512] for i in range(2)], [rb(512), ra(512)]
        yield from pipeline(8, cload, gate, outp, mlp)

    def layer1(b, par):
        phase()
        ra, rb = Cutter(RA, 3 * PADN), Cutter(RB, 2 * L)
        YP = ra(2 * PADN, 96).rearrange("p (j y x) -> p j y x", j=2, y=PADW)
        c1 = rb(864, 96).rearrange("p (t c) -> p t c", t=9)
        c2 = rb(864, 96).rearrange("p (t c) -> p t c", t=9)
        c3 = rb(96, 96)
        dma(("d.w", 0), "w0", c1, A["c1"])
        dma(("d.w", 0), "w0", c2, A["c2"])
        dma(("d.w", 0), "w0", c3, A["c3"])
        mark(("d.rim", 0), borders(YP, 2, 96))
        wait(AC, ("d.rim", 0))
        for i in range(8):
            wait(SP, ("d.in", i - 2))
            dma(("d.x", i), f"xt{i % 2}", XT[:, i % 2, 0, :], x1d[par, 0, :, i * 512:(i + 1) * 512])
            wait(AC, ("d.x", i))
            mark(("d.in", i), act(YP[:, 0, 1 + 8 * i:9 + 8 * i, 1:65],
                                  XT[:, i % 2, 0, :].rearrange("p (y x) -> p y x", y=8), ACT.Identity,
                                  bias=DV0[0:96, 35:36], scale=DV0[0:96, 32:33]))
            yield 0.5
        wait(PE, ("d.w", 0))

        def conv1(i):
            wait(PE, ("d.in", min(i + 1, 7)))
            n, pb = bank()
            mark(("d.c1", i), conv9(pb, 96, lambda tap: c1[:, tap, :], YP[:, 0], i))
            wait(AC, ("d.c1", i))
            mark(("d.y1", i), act(YP[:, 1, 1 + 8 * i:9 + 8 * i, 1:65], pb[0:96, :].rearrange("p (y x) -> p y x", y=8),
                                  ACT.Relu, bias=DV0[0:96, 36:37], scale=DV0[0:96, 33:34]))
            emptied(n, done["d.y1", i])
            yield 7.7

        def conv2(i):
            wait(PE, ("d.y1", min(i + 1, 7)))
            n, pb = bank()
            mark(("d.c2", i), conv9(pb, 96, lambda tap: c2[:, tap, :], YP[:, 1], i))
            wait(AC, ("d.c2", i), ("d.c3", i - 3))
            mark(("d.y2", i), act(T0[0:96, i % 3, :], pb[0:96, :], ACT.Relu, bias=DV0[0:96, 37:38],
                                  scale=DV0[0:96, 34:35]))
            emptied(n, done["d.y2", i])
            yield 7.7

        def conv3(i):
            n, pb = bank()
            wait(PE, ("d.y2", i))
            mark(("d.c3", i), PE.inc(mm(pb[0:96, :], c3, T0[0:96, i % 3, :], True, True)))
            wait(AC, ("d.c3", i), ("d.xlout", i - 3))
            mark(("d.xl", i), act(T1[0:96, i % 3, :], pb[0:96, :], ACT.Relu, bias=vec("c3b")))
            emptied(n, done["d.xl", i])
            yield 0.9
            wait(SP, ("d.xl", i))
            dma(("d.xlout", i), f"t1{i % 3}", xld[par, :, i * 512:(i + 1) * 512], T1[0:96, i % 3, :])
        yield from pipeline(8, conv1, lambda i: iter(()), conv2, conv3)
        phase()
        ra, rb = Cutter(RA, 3 * PADN), Cutter(RB, 2 * L)
        YP = ra(2 * PADN, 96).rearrange("p (j y x) -> p j y x", j=2, y=PADW)
        wip, wig = ra(384, 96), ra(384, 96)
        DG = ra(18 * 96, 96).rearrange("p (t c) -> p t c", t=18)
        ZT, ZO = [ra(512, 96) for _ in range(2)], [XI[0:96, i, :, :].rearrange("p a c -> p (a c)")[:, 0:512] for i in range(2)]
        XM, VR = rb(L, 96), rb(L, 96)
        dma(("e.w", 0), "w0", wip, A["wip"])
        wait(DV, ("e.w", 0))
        mark(("e.wg", 0), DV.inc(nc.vector.tensor_scalar(wig, wip, vec("lng"), None, MUL)))
        n, pb = bank()
        wait(PE, ("e.w", 0))
        for e in range(4):
            t = mm(pb[0:96, e:e + 1], wip[:, e * 96:(e + 1) * 96], vec("lnb"), True, True)
        mark(("e.b", 0), PE.inc(t))
        ipb, ipc = IPW[:, 0:4], IPW[:, 4:8]
        wait(AC, ("e.b", 0))
        mark(("e.ipb", 0), act(ipb, pb[0:96, 0:4], ACT.Copy))
        emptied(n, act(ipc, pb[0:96, 0:4], ACT.Copy, scale=0.5))
        mark(("e.ipc", 0), done["emptied", n])
        w1_ = VCOL["w1"][0]
        for i in range(18):
            mark(("e.diag", 0), PO.inc(nc.gpsimd.tensor_scalar(DG[:, i, :], IDENT[0:96, 0:96],
                                                               V[0:96, w1_ + i:w1_ + i + 1], 1.0, MUL, MUL)))
        mark(("e.rim", 0), borders(YP, 2, 96))
        yield 1

        def nload(i):
            wait(SP, ("e.xm", i - 2))
            dma(("e.x", i), f"xt{i % 2}", XT[:, i % 2, 0, :], x1d[par, 1, :, i * 512:(i + 1) * 512])
            yield 0

        def mean(i):
            cs_ = slice(i * 512, (i + 1) * 512)
            n, pb = bank()
            wait(PE, ("e.x", i))
            mark(("e.mean", i), PE.inc(mm(pb[0:96, :], M96[:, :], XT[:, i % 2, 0, :], True, True)))
            wait(DV, ("e.mean", i))
            mark(("e.xm", i), tt(XM[:, cs_], XT[:, i % 2, 0, :], pb[0:96, :], SUB))
            emptied(n, done["e.xm", i])
            wait(AC, ("e.xm", i), ("e.var", i - 3))
            mark(("e.sq", i), act(T0[0:96, i % 3, :], XM[:, cs_], ACT.Square))
            yield 0.9

        def var(i):
            cs_ = slice(i * 512, (i + 1) * 512)
            n, pb = bank()
            wait(PE, ("e.sq", i))
            mark(("e.var", i), PE.inc(mm(pb[0:96, :], M96[:, :], T0[0:96, i % 3, :], True, True)))
            wait(AC, ("e.var", i))
            mark(("e.vr", i), act(VR[:, cs_], pb[0:96, :], ACT.Copy))
            emptied(n, done["e.vr", i])
            yield 0.9
        yield from pipeline(8, nload, mean, var)
        wait(AC, ("e.vr", 7))
        mark(("e.ln", 0), act(VR, VR, ACT.Ln, bias=ONE[0:96, 1:2]))
        yield 2
        wait(AC, ("e.ln", 0))
        mark(("e.rstd", 0), act(VR, VR, ACT.Exp, scale=-0.5))
        yield 2
        wait(DV, ("e.rstd", 0), ("e.xm", 7))
        wait(PE, ("e.wg", 0), ("e.diag", 0), ("e.rim", 0))
        wait(AC, ("e.ipb", 0), ("e.ipc", 0), ("e.rim", 0))

        def norm(i):
            cs_ = slice(i * 512, (i + 1) * 512)
            wait(DV, ("e.p", 4 * (i - 3) + 3))
            mark(("e.xn", i), tt(T0[0:96, i % 3, :], XM[:, cs_], VR[:, cs_], MUL))
            yield 0

        def inproj(i):
            cs_ = slice(i * 512, (i + 1) * 512)
            wait(PE, ("e.xn", i))
            for e in range(4):
                n, pb = bank()
                mark(("e.p", 4 * i + e), PE.inc(mm(pb[0:96, :], wig[:, e * 96:(e + 1) * 96], T0[0:96, i % 3, :], True, True)))
                if e < 2:
                    wait(AC, ("e.p", 4 * i + e))
                    emptied(n, act(YP[:, e, 1 + 8 * i:9 + 8 * i, 1:65], pb[0:96, :].rearrange("p (y x) -> p y x", y=8),
                                   ACT.Identity, bias=ipb[:, e:e + 1]))
                    mark(("e.rows", i), done["emptied", n])
                else:
                    m = 2 * i + e - 2
                    s_ = m % 2
                    wait(AC, ("e.p", 4 * i + e), ("e.z", m - 2), ("e.zout", m - 2))
                    act(ZT[s_], pb[0:96, :], ACT.Tanh, bias=ipc[:, e:e + 1], scale=0.5)
                    emptied(n, act(ZO[s_], pb[0:96, :], ACT.Identity, bias=ipc[:, e:e + 1], scale=0.5))
                    wait(DV, ("emptied", n))
                    mark(("e.z", m), stt(ZO[s_], ZT[s_], 1.0, ZO[s_], ADD, MUL))
                    wait(SP, ("e.z", m))
                    dma(("e.zout", m), f"xi{s_}", zd[par, e - 2, :, cs_], ZO[s_])
                yield 0.9
        yield from pipeline(8, norm, inproj)
        C1 = RB[0:96, 0:2 * L].rearrange("p (j l) -> p j l", j=2)
        C1T = RB[0:96, 0:2 * L].rearrange("p (j h w) -> p j w h", j=2, h=64)
        wait(DV, ("e.xn", 7))

        def dconv(m):
            j, i = divmod(m, 8)
            wait(PE, ("e.rows", min(i + 1, 7)))
            n, pb = bank()
            mark(("e.conv", m), conv9(pb, 96, lambda tap: DG[:, j * 9 + tap, :], YP[:, j], i))
            yield 7.7
            wait(AC, ("e.conv", m), ("e.silu", m - 3), ("e.p", 31))
            act(T0[0:96, m % 3, :], pb[0:96, :], ACT.Tanh, bias=DV0[0:96, 24 + j:25 + j], scale=0.5)
            emptied(n, act(T1[0:96, m % 3, :], pb[0:96, :], ACT.Identity, bias=DV0[0:96, 24 + j:25 + j], scale=0.5))
            wait(DV, ("emptied", n))
            mark(("e.silu", m), stt(C1[:, j, i * 512:(i + 1) * 512], T0[0:96, m % 3, :], 1.0, T1[0:96, m % 3, :], ADD, MUL))
            yield 0
        yield from pipeline(16, dconv)
        phase()
        ra = Cutter(RA, 3 * PADN)
        HW_ = 1024
        R0, E0, X0, Y0, X1, E1 = ([ra(HW_, 96) for _ in range(n_)] for n_ in (2, 2, 1, 2, 1, 0))
        XD = [ra(512, 38) for _ in range(8)]
        xpw = ra(304, 96).rearrange("p (m k c) -> p m k c", m=2, k=4)
        dtw = WD[:, :].rearrange("p (k c) -> p k c", k=4)
        dma(("f.w", 0), "w0", xpw, A["xpw"])
        for j in range(2):
            dma(("f.xcout", 0), "w1", xcd[par, j], C1[:, j, :])
        wait(PE, ("f.w", 0))
        for k in range(4):
            for i in range(8):
                n_ = 8 * k + i
                cs_ = slice(i * 512, (i + 1) * 512)
                n, pb = bank()
                for m in range(2):
                    x_ = C1[:, m, cs_] if k % 2 == 0 else C1T[:, m, 8 * i:8 * i + 8, :]
                    t = mm(pb[0:38, :], xpw[:, m, k, :], x_, m == 0, m == 1)
                mark(("f.xp", n_), PE.inc(t))
                wait(AC, ("f.xp", n_), ("f.xdout", n_ - 8), ("f.dt", 8 * (2 * k - 1) + i))
                mark(("f.xd", n_), act(XD[i], pb[0:38, :], ACT.Copy))
                emptied(n, done["f.xd", n_])
                yield 1.7
                wait(SP, ("f.xd", n_))
                dma(("f.xdout", n_), f"xd{i}", bcd[par, k, :, cs_], XD[i][6:38, :])

            def steps(v_):
                m, q4 = divmod(v_, 4)
                u = 8 * k + v_
                bias = vec("dtb1", k * 2 + m)
                r_, e_ = R0[u % 2], E0[u % 2]
                wait(AC, ("f.du", u - 2), ("f.x1", 2 * (u - 2)), ("f.pr", 2 * (u - 2)), ("f.pe", 2 * (u - 2) + 1))
                for i in range(2):
                    t_ = 2 * q4 + i
                    o = slice(i * 512, (i + 1) * 512)
                    n, pb = bank()
                    wait(PE, ("f.xd", 8 * k + t_))
                    key = 8 * (2 * k + m) + t_
                    mark(("f.dt", key), PE.inc(mm(pb[0:96, :], dtw[:, k, m * 96:(m + 1) * 96], XD[t_][0:6, :], True, True)))
                    wait(AC, ("f.dt", key))
                    mark(("f.abs", u), act(e_[:, o], pb[0:96, :], ACT.Abs, bias=bias))
                    emptied(n, act(r_[:, o], pb[0:96, :], ACT.Relu, bias=bias))
                    yield 0.9
                mark(("f.relu", u), done["emptied", n])
                wait(AC, ("f.abs", u))
                mark(("f.exp", u), act(e_, e_, ACT.Exp, scale=-1.0))
                yield 0.5

            def logs(pair):
                for v_ in (2 * pair, 2 * pair + 1):
                    u = 8 * k + v_
                    wait(AC, ("f.exp", u))
                    mark(("f.ln", u), act(E0[u % 2], E0[u % 2], ACT.Ln, bias=ONE[0:96, 0:1]))

            def split(v_):
                m, q4 = divmod(v_, 4)
                u = 8 * k + v_
                ms = slice(m * 96, (m + 1) * 96)
                hs = slice(q4 * HW_, (q4 + 1) * HW_)
                r_, e_, y_ = R0[u % 2], E0[u % 2], Y0[u % 2]
                wait(DV, ("f.ln", u), ("f.relu", u))
                mark(("f.sum", u), tt(r_, r_, e_, ADD))
                wait(DV, ("f.sum", u), ("f.pr", 2 * (u - 2) + 1), ("f.x1", 2 * (u - 2) + 1))
                if k % 2 == 0:
                    mark(("f.du", u), tt(y_, r_, C1[:, m, hs], MUL))
                else:
                    mark(("f.du", u), tt(y_.rearrange("p (w h) -> p w h", h=64), r_.rearrange("p (w h) -> p w h", h=64),
                                         C1T[:, m, q4 * 16:(q4 + 1) * 16, :], MUL))
                yield 1
                for which, s_, src in ((0, r_, ("f.sum", u)), (1, y_, ("f.du", u))):
                    v2 = 2 * u + which
                    x_ = (X0 + X1)[which]
                    wait(DV, src, ("f.x2", v2 - 2), ("f.px", v2 - 2))
                    mark(("f.x1", v2), tt(x_, s_, hi(s_), SUB))
                    wait(PO, ("f.x1", v2), ("f.pe", v2 - 1))
                    mark(("f.x2", v2), ptt(e_, x_, hi(x_), SUB))
                    yield 0.5
                    dst = ptd[par, k, 3 * m:3 * m + 3, :, which, hs]
                    wait(SP, ("f.x1", v2))
                    dma(("f.pr", v2), f"pr{which}{u % 2}", dst[:, 0:32, :], s_)
                    dma(("f.px", v2), f"px{which}", dst[:, 32:64, :], x_)
                    wait(SP, ("f.x2", v2))
                    dma(("f.pe", v2), f"pe{u % 2}", dst[:, 64:96, :], e_)
                    yield 0.5
            for pair in range(4):
                yield from steps(2 * pair)
                yield from steps(2 * pair + 1)
                logs(pair)
                yield from split(2 * pair)
                yield from split(2 * pair + 1)

    def scan(b, par):
        units = [(k, c, d, g) for k in range(4) for c in (range(4) if k < 2 else range(3, -1, -1))
                 for d in range(6) for g in range(4)]
        N = len(units)

        def fetch_bc(v):
            k, c, _, _ = units[24 * v]
            cs_ = slice(c * 1024, (c + 1) * 1024)
            wait(SP, ("S.mulC", 24 * (v - NBR) + 23))
            for w in range(2):
                dma(("S.bc", v), f"Sbc{v % NBR}", BR[:, v % NBR, w, :],
                    bcd[par, k, w * 16:w * 16 + 16, cs_].unsqueeze(0).to_broadcast([8, 16, 1024]))

        def fetch_pt(v):
            k, c, d, _ = units[4 * v]
            wait(SP, ("S.PU", 4 * (v - NPT) + 3))
            dma(("S.pt", v), f"Spt{v % NPT}", PT[:, v % NPT, :, :], ptd[par, k, d, :, :, c * 1024:(c + 1) * 1024])

        def expand(u, which, P, key):
            g = units[u][3]
            for q in range(2):
                t = mm(P[:, q * 512:(q + 1) * 512], SEL[:, g, :], hi(PT[:, (u // 4) % NPT, which, q * 512:(q + 1) * 512]),
                       True, True)
            mark((key, u), PE.inc(t))

        def decay(u):
            k, c, d, g = units[u]
            wait(PE, ("S.pt", u // 4), ("S.exp", u - 1))
            expand(u, 0, PD, "S.PD")
            ai = k * 24 + d * 4 + g
            wait(AC, ("S.PD", u), ("S.scan", u - NA))
            mark(("S.exp", u), act(dA[:, u % NA, :], PD[:, :], ACT.Exp, scale=A1[:, ai:ai + 1]))

        def drive(u):
            wait(PE, ("S.mulB", u - 1))
            expand(u, 1, PU, "S.PU")
            wait(DV, ("S.PU", u), ("S.bc", u // 24), ("S.mulC", u - NH), ("S.last", (u - NH) | 1 if u >= NH else -1))
            mark(("S.mulB", u), tt(H[:, u % NH, :], PU[:, :], BR[:, (u // 24) % NBR, 0, :], MUL))

        def scan_(u):
            k, c, d, g = units[u]
            gi = d * 4 + g
            first = c == (0 if k < 2 else 3)
            h, a_ = H[:, u % NH, :], dA[:, u % NA, :]
            wait(DV, ("S.exp", u), ("S.mulB", u))
            if not first:
                wait(DV, ("S.last", (u - 24) | 1))
            init = 0.0 if first else CR[:, gi:gi + 1]
            if k >= 2:
                h, a_ = h[:, ::-1], a_[:, ::-1]
            mark(("S.scan", u), DV.inc(nc.vector.tensor_tensor_scan(h, a_, h, init, MUL, ADD)))
            if u % 2 == 1:
                s0 = (u - 1) % NH
                wait(AC, ("S.scan", u))
                mark(("S.last", u), act(CR[:, gi - 1:gi + 1], H[:, s0:s0 + 2, 1023 if k < 2 else 0], ACT.Copy))
            wait(PO, ("S.scan", u), ("S.sum", u - NHC))
            mark(("S.mulC", u), ptt(HC[:, u % NHC, :], H[:, u % NH, :], BR[:, (u // 24) % NBR, 1, :], MUL))

        def total(u):
            k, c, d, g = units[u]
            v = u // 4
            wait(PE, ("S.mulC", u), ("S.y", v - 1))
            for q in range(4):
                t = mm(PY[32 * q:32 * q + 32, :], RED[:, g, :], HC[:, u % NHC, q * 256:(q + 1) * 256], g == 0, g == 3)
            mark(("S.sum", u), PE.inc(t))
            if g == 3:
                wait(AC, ("S.sum", u), ("S.yout", v - 2))
                mark(("S.y", v), act(YS[:, v % 2, :], PY[:, :], ACT.Copy))

        def put(v):
            k, c, d, _ = units[4 * v]
            wait(SP, ("S.y", v))
            dma(("S.yout", v), f"Syo{v % 2}", yd[par, k, d, c], YS[:, v % 2, :])

        fetch_bc(0)
        fetch_pt(0)
        fetch_bc(1)
        fetch_pt(1)
        decay(0)
        for u in range(N + 4):
            if u < N:
                drive(u)
            if u >= 3 and u - 3 < N:
                total(u - 3)
            if 1 <= u <= N:
                scan_(u - 1)
            if u + 1 < N:
                decay(u + 1)
            if u % 4 == 0 and NPT <= u // 4 + 1 < N // 4:
                fetch_pt(u // 4 + 1)
            if u % 4 == 3 and u > 3:
                put(u // 4 - 1)
            if u % 24 == 3 and (v := u // 24 + 1) >= NBR and 24 * v < N:
                fetch_bc(v)
            yield 1

    def finish(b, par):
        phase()
        ra, rb = Cutter(RA, 3 * PADN), Cutter(RB, 2 * L)
        XM = ra(2 * L, 96).rearrange("p (j l) -> p j l", j=2)
        VR = ra(L, 96)
        Y13 = rb(2 * L, 96).rearrange("p (j l) -> p j l", j=2)
        Y13v = RB[0:96, 0:2 * L].rearrange("p (j w h) -> p j h w", j=2, w=64)

        def halves(k, j, cc):
            return [yd[par, k, 3 * j + g, cc].rearrange("c (q r) n -> r (c q) n", q=4) for g in range(3)]

        for j in range(2):
            for g in range(3):
                for (k, dst) in ((1, XM), (3, Y13)):
                    dma((f"g.y{k}", 0), f"w{k}", dst[32 * g:32 * g + 32, j, :].rearrange("p (a n) -> p a n", n=256),
                        yd[par, k, 3 * j + g].rearrange("c (q r) n -> r (c q) n", q=4))
        for i in range(8):
            wait(PO, ("g.y1", 0), ("g.y3", 0))
            s_ = slice(i * 1024, (i + 1) * 1024)
            mark(("g.y13", 0), ptt(RB[0:96, s_], RB[0:96, s_], RA[0:96, s_], ADD))
            yield 1
        BA, BB = B2, X2

        def gload(i):
            cs_ = slice(i * 512, (i + 1) * 512)
            wait(SP, ("g.xm", i - 2), ("g.mean", i - 2), ("g.y02", i - 1), ("g.d", i - 1))
            for k, dst, nm in ((0, XT[:, i % 2], f"xt{i % 2}"), (2, BA, "b2")):
                for j in range(2):
                    for g in range(3):
                        src = yd[par, k, 3 * j + g, i // 2].rearrange("(q r) n -> r q n", q=4)[:, 2 * (i % 2):2 * (i % 2) + 2, :]
                        dma((f"g.y{k}", i), nm, dst[32 * g:32 * g + 32, j, :].rearrange("p (a n) -> p a n", n=256), src)
            dma(("g.xc", i), "x2", BB[:, :, :], xcd[par, :, :, cs_].rearrange("j p n -> p j n"))
            yield 0

        def total(i):
            cs_ = slice(i * 512, (i + 1) * 512)
            a_ = XT[:, i % 2]
            wait(DV, ("g.y0", i), ("g.y2", i), ("g.y13", 0))
            mark(("g.y02", i), tt(a_, a_, BA[:, :, :], ADD))
            wait(DV, ("g.y02", i))
            for j in range(2):
                v = a_[:, j, :].rearrange("p (h w) -> p h w", h=8)
                mark(("g.yall", i), tt(v, v, Y13v[:, j, 8 * i:8 * i + 8, :], ADD))
            wait(DV, ("g.yall", i), ("g.xc", i))
            for j in range(2):
                mark(("g.d", i), stt(a_[:, j, :], BB[:, j, :], DV0[0:96, 30 + j:31 + j], a_[:, j, :], MUL, ADD))
            yield 1

        def mean(i):
            cs_ = slice(i * 512, (i + 1) * 512)
            a_ = XT[:, i % 2]
            n, pb = bank()
            wait(PE, ("g.d", i))
            for j in range(2):
                t = mm(pb[0:96, :], M192[:, :], a_[:, j, :], j == 0, j == 1)
            mark(("g.mean", i), PE.inc(t))
            wait(DV, ("g.mean", i), ("g.d", i))
            for j in range(2):
                mark(("g.xm", i), tt(XM[:, j, cs_], a_[:, j, :], pb[0:96, :], SUB))
            emptied(n, done["g.xm", i])
            yield 1
            wait(AC, ("g.xm", i), ("g.var", i - 1))
            for j in range(2):
                mark(("g.sq", i), act(T0[0:96, j, :], XM[:, j, cs_], ACT.Square))
            yield 1

        def var(i):
            cs_ = slice(i * 512, (i + 1) * 512)
            n, pb = bank()
            wait(PE, ("g.sq", i))
            for j in range(2):
                t = mm(pb[0:96, :], M192[:, :], T0[0:96, j, :], j == 0, j == 1)
            mark(("g.var", i), PE.inc(t))
            wait(AC, ("g.var", i))
            mark(("g.vr", i), act(VR[:, cs_], pb[0:96, :], ACT.Copy))
            emptied(n, done["g.vr", i])
            yield 1
        yield from pipeline(8, gload, total, mean, var)
        wait(AC, ("g.vr", 7))
        mark(("g.ln", 0), act(VR, VR, ACT.Ln, bias=ONE[0:96, 1:2]))
        yield 2
        wait(AC, ("g.ln", 0))
        mark(("g.rstd", 0), act(VR, VR, ACT.Exp, scale=-0.5))
        yield 2
        ov = A["out"][b].rearrange("(i q p) c -> i p q c", q=4, p=128)
        wait(DV, ("g.rstd", 0), ("g.xm", 7))
        ZB = [rb_ for rb_ in (RB[0:96, 0:1024], RB[0:96, 1024:2048])]
        XB = [rb_ for rb_ in (RB[0:96, 2048:3072], RB[0:96, 3072:4096])]
        LB = [rb_ for rb_ in (RB[0:96, 4096:4608], RB[0:96, 4608:5120])]
        wait(SP, ("g.yall", 7), ("g.mean", 7), ("g.d", 7))

        def hload(i):
            cs_ = slice(i * 512, (i + 1) * 512)
            wait(SP, ("h.gate", 2 * (i - 2) + 1), ("h.mm", 2 * (i - 2) + 1))
            dma(("h.z", i), f"hz{i % 2}", ZB[i % 2].rearrange("p (j n) -> p j n", j=2),
                zd[par, :, :, cs_].rearrange("j p n -> p j n"))
            dma(("h.x", i), f"hx{i % 2}", XB[i % 2].rearrange("p (j n) -> p j n", j=2),
                x1d[par, :, :, cs_].rearrange("j p n -> p j n"))
            dma(("h.l", i), f"hl{i % 2}", LB[i % 2], xld[par, :, cs_])
            yield 0

        def gates(i):
            cs_ = slice(i * 512, (i + 1) * 512)
            for j in range(2):
                m = 2 * i + j
                o = XT[:, i % 2, j, :]
                wait(DV, ("h.mm", 2 * (i - 2) + 1))
                mark(("h.n", m), tt(o, XM[:, j, cs_], VR[:, cs_], MUL))
                wait(AC, ("h.n", m))
                mark(("h.g", m), act(o, o, ACT.Identity, bias=vec("onb", j), scale=vec("ong", j)))
                yield 1
                wait(DV, ("h.g", m), ("h.z", i))
                mark(("h.gate", m), tt(o, o, ZB[i % 2][:, j * 512:(j + 1) * 512], MUL))

        def final(i):
            wait(PE, ("h.gate", 2 * i + 1), ("h.x", i), ("h.l", i))
            for q2 in range(2):
                n, pb = bank()
                for q in range(2):
                    o = pb[:, q * 192:(q + 1) * 192]
                    s_ = slice((q2 * 2 + q) * 128, (q2 * 2 + q + 1) * 128)
                    s1 = slice(512 + (q2 * 2 + q) * 128, 512 + (q2 * 2 + q + 1) * 128)
                    mm(o, XT[:, i % 2, 0, s_], WP[:, 0:192], True, False)
                    mm(o, XT[:, i % 2, 1, s_], WP[:, 192:384], False, False)
                    mm(o, LB[i % 2][:, s_], PERM[:, 0:192], False, False)
                    mm(o, XB[i % 2][:, s_], PERM[:, 384:576], False, False)
                    t = mm(o, XB[i % 2][:, s1], PERM[:, 576:768], False, True)
                mark(("h.mm", 2 * i + q2), PE.inc(t))
                wait(AC, ("h.mm", 2 * i + q2), ("h.out", i - 2))
                emptied(n, act(XI[:, i % 2, 2 * q2:2 * q2 + 2, :], pb[:, 0:384].rearrange("p (q c) -> p q c", q=2),
                               ACT.Copy))
                yield 3.2
            wait(SP, ("emptied", n))
            dma(("h.out", i), f"xi{i % 2}", ov[i], XI[:, i % 2, :, :])
        yield from pipeline(8, hload, gates, final)

    B2 = sb("B2", [96, 2, 512])
    X2 = sb("X2", [96, 2, 512])

    def reset():
        for n in lanes:
            if count[n]:
                nc.sync.wait_ge(lanes[n], count[n])
        nc.all_engine_barrier()
        for s_ in [e.sem for e in engines] + list(lanes.values()):
            nc.gpsimd.sem_clear(s_)
        nc.all_engine_barrier()
        done.clear()
        bank_no[0] = 0
        for e in engines:
            e.n = 0
        for n in count:
            count[n] = 0

    def chain(*gens):
        for g in gens:
            yield from g

    def run(gen):
        t = 0
        for c in gen:
            t += c
        return t

    def beside(s_gen, d_gen, total_):
        at, n = 0.0, 0
        spent = 0.0
        for _ in s_gen:
            n += 1
            while at < total_ * n / 384:
                c = next(d_gen, None)
                if c is None:
                    at = float("inf")
                    break
                at += c
                spent += c
        spent += run(d_gen)
        return spent

    setup()
    reset()
    run(chain(layer0(0, 0), layer1(0, 0)))
    reset()
    PRE, FIN = 1338.0, 111.0
    beside(scan(0, 0), chain(layer0(1, 1), layer1(1, 1)), PRE)
    reset()
    if NB > 2:
        with nc.Fori(1, NB - 2, 2) as i:
            for o in range(2):
                p = (1 + o) % 2
                beside(scan(i + o, p), chain(finish(i + (o - 1), 1 - p), layer0(i + (o + 1), 1 - p),
                                             layer1(i + (o + 1), 1 - p)), PRE + FIN)
                reset()
    beside(scan(NB - 1, 1), finish(NB - 2, 0), FIN)
    reset()
    run(finish(NB - 1, 1))
    reset()


def _consts():
    c = np.zeros((128, NC_), np.float32)

    def put(name, a):
        x, _ = CCOL[name]
        c[:a.shape[0], x:x + a.shape[1]] = a
    put("ident", np.eye(128, dtype=np.float32))
    i = np.arange(128)
    put("tri", (i[:, None] <= i[None, :]).astype(np.float32))
    put("ones", np.ones((128, 128), np.float32))
    red = np.zeros((128, 4, 32), np.float32)
    sel = np.zeros((96, 4, 128), np.float32)
    for g in range(4):
        for d in range(8):
            for n in range(16):
                red[d * 16 + n, g, g * 8 + d] = 1
                for part in range(3):
                    sel[part * 32 + g * 8 + d, g, d * 16 + n] = 1
    put("red", red.reshape(128, 128))
    put("sel", sel.reshape(96, 512))
    put("neg", np.where(i[None, :] >= i[:, None], 0.0, -1e30).astype(np.float32))
    one3 = np.zeros((96, 32), np.float32)
    one3[0:3] = 1
    put("one3", one3)
    perm = np.zeros((96, 768), np.float32)
    for j in range(96):
        perm[j, 2 * j] = 1
        perm[j, 192 + 2 * j + 1] = 1
        perm[j, 384 + j] = 1
        perm[j, 576 + 96 + j] = 1
    put("perm", perm)
    return c


def _layouts(a, NB):
    def cols(x, P):
        return np.asarray(x).reshape(-1, P).T
    v = np.zeros((128, NV), np.float32)

    def put(name, x):
        lo, hi_ = VCOL[name]
        assert x.shape[1] == hi_ - lo, name
        v[:x.shape[0], lo:hi_] = x
    p0, p1 = "L0_conv_", "L1_conv_"
    put("cb", cols(a[p0 + "conv_b"], 128))
    put("ds0", cols(np.repeat(a[p0 + "Ds"], 64), 128))
    put("b1", cols(a[p0 + "b1"], 128))
    put("b2", cols(a[p0 + "b2"], 96))
    put("alog0", np.broadcast_to(a[p0 + "A_logs"], (128, 12)))
    put("dtb0", np.broadcast_to(a[p0 + "dt_bias"], (128, 12)))
    for i in (1, 2, 3):
        put(f"bn{i}", np.stack([a[f"{p1}bn{i}_{q}"] for q in "gbmv"], 1))
        put(f"c{i}b", cols(a[f"{p1}conv{i}_b"], 96))
    put("lng", cols(a[p1 + "ln_g"], 96))
    put("lnb", cols(a[p1 + "ln_b"], 96))
    put("cdb", cols(a[p1 + "conv2d_b"], 96))
    put("dtb1", cols(a[p1 + "dt_proj_b"], 96))
    put("ds1", cols(a[p1 + "Ds"], 96))
    put("ong", cols(a[p1 + "out_norm_g"], 96))
    put("onb", cols(a[p1 + "out_norm_b"], 96))
    put("alog1", a[p1 + "A_logs"].reshape(4, 24, 8, 16).transpose(2, 3, 0, 1).reshape(128, 96))
    put("w0", a[p0 + "conv_w"].reshape(3, 128, 9).transpose(1, 0, 2).reshape(128, 27))
    put("w1", a[p1 + "conv2d_w"].reshape(9, 2, 96).transpose(2, 1, 0).reshape(96, 18))
    o = {"vecs": v, "consts": _consts()}
    o["x"] = a["x"].reshape(8, L, 192)[:NB]
    o["win"] = a[p0 + "W_in"].T.reshape(2, 96, 768).transpose(1, 0, 2)
    xp = a[p0 + "x_proj_weight"]
    xp = np.concatenate([xp[:, 32:64], xp[:, 0:32], xp[:, 64:70]], 1)
    o["wxp0"] = xp.transpose(2, 0, 1).reshape(3, 128, 2, 70).transpose(1, 0, 2, 3)
    o["h0"] = a[p0 + "init_states"].transpose(2, 0, 1).reshape(32, 768)
    o["wout0"] = a[p0 + "W_out"].T.reshape(3, 128, 192).transpose(1, 0, 2)
    o["w1"] = a[p0 + "W1"].T.reshape(2, 96, 768).transpose(1, 0, 2)
    o["w2"] = a[p0 + "W2"].T.reshape(6, 128, 192).transpose(1, 0, 2)
    o["c1"] = a[p1 + "conv1_w"].reshape(9, 96, 96).transpose(1, 0, 2)
    o["c2"] = a[p1 + "conv2_w"].reshape(9, 96, 96).transpose(1, 0, 2)
    o["c3"] = a[p1 + "conv3_w"].reshape(96, 96)
    o["wip"] = a[p1 + "in_proj_w"].T
    o["xpw"] = a[p1 + "x_proj_w"].transpose(2, 0, 1).reshape(2, 96, 4, 38).transpose(1, 0, 2, 3)
    o["dtw"] = a[p1 + "dt_proj_w"].transpose(2, 0, 1)
    wop = np.zeros((96, 2, 192), np.float32)
    wop[:, :, 1::2] = a[p1 + "out_proj_w"].T.reshape(2, 96, 96).transpose(1, 0, 2)
    o["wop"] = wop.reshape(96, 384)
    return {k: np.ascontiguousarray(x, dtype=np.float32) for k, x in o.items()}


def kernel(**inputs):
    import concourse.bacc as _bacc
    from concourse import mybir as _mybir
    from concourse.bass_utils import run_bass_kernel_spmd as _run

    NB = 8
    nc = _bacc.Bacc("TRN2", target_bir_lowering=False, num_devices=1)
    arrays = {f"in_{k}": x for k, x in _layouts({k: np.asarray(x) for k, x in inputs.items()}, NB).items()}
    A = {k[3:]: nc.dram_tensor(k, x.shape, _mybir.dt.from_np(x.dtype), kind="ExternalInput").ap()
         for k, x in arrays.items()}
    A["out"] = nc.dram_tensor("out_0", (NB, L, 192), F32, kind="ExternalOutput").ap()
    program(nc, A, NB)
    r = _run(nc, [arrays], core_ids=[0])
    return r.results[0]["out_0"].reshape(NB, 64, 64, 192)
```

```python
from contextlib import ExitStack

import numpy as np

import concourse.bass as bass
from concourse import mybir

F32 = mybir.dt.float32
BF = mybir.dt.bfloat16
ALU = mybir.AluOpType
ACT = mybir.ActivationFunctionType

L = 4096
PADW = 66
PADN = PADW * PADW
MUL, ADD, SUB, MAX = ALU.mult, ALU.add, ALU.subtract, ALU.max

VCOL = {}
_at = 0
for _name, _n in [("cb", 3), ("ds0", 6), ("b1", 6), ("b2", 2), ("alog0", 12), ("dtb0", 12),
                  ("bn1", 4), ("bn2", 4), ("bn3", 4), ("c1b", 1), ("c2b", 1), ("c3b", 1),
                  ("lng", 1), ("lnb", 1), ("cdb", 2), ("dtb1", 8), ("ds1", 8), ("ong", 2),
                  ("onb", 2), ("alog1", 96), ("w0", 27), ("w1", 18)]:
    VCOL[_name] = (_at, _at + _n)
    _at += _n
NV = _at

CCOL = {}
_at = 0
for _name, _n in [("ident", 128), ("tri", 128), ("ones", 128), ("red", 128), ("sel", 512),
                  ("neg", 128), ("one3", 32), ("perm", 768)]:
    CCOL[_name] = (_at, _at + _n)
    _at += _n
NC_ = _at


NTAP = 6
W_SSD, W_F, W_CHAIN = 0.7, 1.0, 0.5


class Eng:

    def __init__(self, e, sem):
        self.e, self.sem, self.n = e, sem, 0

    def inc(self, inst):
        inst.then_inc(self.sem, 1)
        self.n += 1
        return (self.sem, self.n)


def program(nc, A, NB):
    with ExitStack() as ctx:
        _program(nc, A, NB, ctx)


def _program(nc, A, NB, ctx):
    def sb(n, s, d=F32):
        return ctx.enter_context(nc.sbuf_tensor(n, s, d))

    def ps(n, s):
        return ctx.enter_context(nc.psum_tensor(n, s, F32))

    def sem(n):
        return ctx.enter_context(nc.semaphore(n))

    PE, AC, DV, PO, SP = (Eng(e, sem(n)) for e, n in (
        (nc.tensor, "s_pe"), (nc.scalar, "s_act"), (nc.vector, "s_dve"), (nc.gpsimd, "s_pool"),
        (nc.sync, "s_sp")))
    engines = [PE, AC, DV, PO, SP]

    done = {}
    lanes, count = {}, {}

    def wait(eng, *steps):
        for key in steps:
            if key in done:
                eng.e.wait_ge(*done[key])
            else:
                assert key[-1] < 0, key

    def mark(key, token):
        done[key] = token

    def dma(key, lane, out, in_):
        if lane not in lanes:
            lanes[lane], count[lane] = sem(f"d_{lane}"), 0
        nc.sync.dma_start(out, in_).then_inc(lanes[lane], 16)
        count[lane] += 16
        done[key] = (lanes[lane], count[lane])

    def mm(out, w, x, start, stop):
        return nc.tensor.matmul(out, w, x, start=start, stop=stop, skip_group_check=True)

    def act(out, in_, f, **kw):
        return AC.inc(nc.scalar.activation(out, in_, f, **kw))

    def tt(out, a, b, op):
        return DV.inc(nc.vector.tensor_tensor(out, a, b, op))

    def stt(out, a, s_, b, op0, op1):
        return DV.inc(nc.vector.scalar_tensor_tensor(out, a, s_, b, op0, op1))

    def ptt(out, a, b, op):
        return PO.inc(nc.gpsimd.tensor_tensor(out, a, b, op))

    def dram(n, s, d=F32):
        return nc.dram_tensor(n, s, d).ap()
    xTd = dram("xTd", (2, 96, L))
    xc0 = dram("xc0", (3, 128, L))
    tkd = dram("tkd", (L, 524))
    dtd = dram("dtd", (L, 12))
    y0d = dram("y0d", (2, L, 384))
    spd = dram("spd", (3, 384, 128), BF)
    x1d = dram("x1d", (2, 2, 96, L))
    xld = dram("xld", (2, 96, L))
    zd = dram("zd", (2, 2, 96, L))
    xcd = dram("xcd", (2, 2, 96, L))
    ptd = dram("ptd", (2, 4, 6, 96, 2, L), BF)
    bcd = dram("bcd", (2, 4, 32, L))
    yd = dram("yd", (2, 4, 6, 4, 128, 256))

    RA = sb("RA", [128, 3 * PADN])
    RB = sb("RB", [128, 2 * L])
    WD = sb("WD", [38, 384])
    IPW = sb("IPW", [96, 8])
    WP = sb("WP", [96, 384])
    PERM = sb("PERM", [96, 768])
    CB = sb("CB", [128, 512])
    SELB = sb("SELB", [96, 512], BF)
    NEGB = sb("NEGB", [128, 128], BF)
    IDB = sb("IDB", [128, 128], BF)
    V = sb("V", [128, NV])
    DV0 = sb("DV0", [128, 48])
    A1 = sb("A1", [128, 96])
    M96 = sb("M96", [96, 96])
    M192 = sb("M192", [96, 96])
    ONE = sb("ONE", [128, 2])
    WH = sb("WH", [128, 45])
    IDENT = CB[:, 0:128]
    TRI = CB[:, 128:256]
    ONES = CB[:, 256:384]
    RED = CB[:, 384:512].rearrange("p (g c) -> p g c", g=4)
    SEL = SELB[:, :].rearrange("p (g c) -> p g c", g=4)

    def vec(name, i=0, n=1, P=96):
        a = VCOL[name][0] + i
        return V[0:P, a:a + n]

    NA, NH, NHC, NBR, NPT = 3, 4, 3, 2, 2
    dA = sb("dA", [128, NA, 1024])
    H = sb("H", [128, NH, 1024])
    HC = sb("HC", [128, NHC, 1024])
    BR = sb("BR", [128, NBR, 2, 1024])
    PT = sb("PT", [96, NPT, 2, 1024], BF)
    CR = sb("CR", [128, 24])
    YS = sb("YS", [128, 2, 256])
    PD = ps("PD", [128, 512])
    PU = ps("PU", [128, 1024])
    PY = ps("PY", [128, 256])
    NP = 4
    PB = [ps(f"PB{i}", [128, 512]) for i in range(NP)]
    T0 = sb("T0", [128, 3, 512])
    T1 = sb("T1", [128, 3, 512])
    XT = sb("XT", [96, 2, 2, 512])
    XI = sb("XI", [128, 2, 4, 192])
    B2 = sb("B2", [96, 2, 512])
    X2 = sb("X2", [96, 2, 512])
    PX = sb("PX", [128, 3072])

    bank_no = [0]

    def bank():
        n = bank_no[0]
        bank_no[0] += 1
        wait(PE, ("emptied", n - NP))
        return n, PB[n % NP]

    def emptied(n, token):
        mark(("emptied", n), token)

    def phase():
        for eng in (AC, DV, PO, SP):
            for e in (PE, AC, DV, PO):
                if e.n:
                    eng.e.wait_ge(e.sem, e.n)
            for n in lanes:
                if n[0] != "S" and count[n]:
                    eng.e.wait_ge(lanes[n], count[n])

    class Cutter:

        def __init__(self, t, size):
            self.t, self.size, self.at = t, size, 0

        def __call__(self, n, P=128):
            a = self.at
            self.at += n
            assert self.at <= self.size, (self.at, self.size)
            return self.t[0:P, a:a + n]

    def pipeline(n, *stages):
        for r in range(n + len(stages) - 1):
            for s_ in range(len(stages) - 1, -1, -1):
                if 0 <= r - s_ < n:
                    yield from stages[s_](r - s_)

    def woven(n, load, *stages):
        for r in range(n + len(stages)):
            gens = [stages[s_](r - s_ - 1) for s_ in range(len(stages) - 1, -1, -1) if 0 <= r - s_ - 1 < n]
            while gens:
                for g in list(gens):
                    c = next(g, None)
                    if c is None:
                        gens.remove(g)
                    else:
                        yield c
            if r < n:
                yield from load(r)

    def idle(i):
        return iter(())

    def scaled(f, gen):
        for c in gen:
            yield f * c

    def setup():
        dma(("consts", 0), "c0", RA[:, 0:NC_], A["consts"])
        dma(("vecs", 0), "c1", V[:, :], A["vecs"])
        dma(("weights", 0), "c2", WP[:, :], A["wop"])
        for i in range(2):
            dma(("weights", 0), "c2", WD[32 * i:32 * i + 6, :].rearrange("r (k c) -> r k c", k=2), A["dtw"][:, 2 * i:2 * i + 2, :])
        v = nc.vector

        def c(name, P=128):
            x, y = CCOL[name]
            return RA[0:P, x:y]
        wait(DV, ("consts", 0), ("vecs", 0))
        v.tensor_copy(CB[:, :], RA[:, 0:512])
        v.tensor_copy(SELB[:, :], c("sel", 96))
        v.tensor_copy(NEGB[:, :], c("neg"))
        v.tensor_copy(IDB[:, :], c("ident"))
        v.tensor_copy(PERM[:, :], c("perm", 96))
        v.memset(M96[:, :], 1.0 / 96)
        v.memset(M192[:, :], 1.0 / 192)
        v.memset(ONE[:, 0:1], 1.0)
        v.memset(ONE[:, 1:2], 1e-5)
        wait(AC, ("vecs", 0))
        a0 = VCOL["alog1"][0]
        act(A1[:, :], V[:, a0:a0 + 96], ACT.Exp)
        a0 = VCOL["alog0"][0]
        mark(("exps", 0), act(DV0[:, 0:12], V[:, a0:a0 + 12], ACT.Exp))
        wait(DV, ("exps", 0))
        v.tensor_scalar(A1[:, :], A1[:, :], -1.0, None, MUL)
        v.tensor_scalar(DV0[:, 0:12], DV0[:, 0:12], -1.0, None, MUL)
        d0 = VCOL["ds0"][0]
        v.tensor_tensor(DV0[:, 12:15], V[:, d0:d0 + 3], V[:, d0 + 3:d0 + 6], ADD)
        c0 = VCOL["cb"][0]
        v.tensor_scalar(DV0[:, 15:18], V[:, c0:c0 + 3], 0.5, None, MUL)
        c0 = VCOL["b1"][0]
        v.tensor_scalar(DV0[:, 18:24], V[:, c0:c0 + 6], 0.5, None, MUL)
        for i, nm in enumerate(("w0", "w1")):
            c0, c1_ = VCOL[nm]
            v.tensor_scalar(WH[:, 27 * i:27 * i + c1_ - c0], V[:, c0:c1_], 0.5, None, MUL)
        c0 = VCOL["cdb"][0]
        v.tensor_scalar(DV0[0:96, 24:26], V[0:96, c0:c0 + 2], 0.5, None, MUL)
        c0 = VCOL["ds1"][0]
        mark(("ds", 0), tt(DV0[0:96, 26:30], V[0:96, c0:c0 + 4], V[0:96, c0 + 4:c0 + 8], ADD))
        wait(DV, ("ds", 0))
        v.tensor_tensor(DV0[0:96, 30:32], DV0[0:96, 26:28], DV0[0:96, 28:30], ADD)
        for i in range(3):
            q = VCOL[f"bn{i + 1}"][0] + 3
            mark(("v+eps", 0), DV.inc(v.tensor_scalar(DV0[0:96, 38 + i:39 + i], V[0:96, q:q + 1], 1e-5, None, ADD)))
        wait(AC, ("v+eps", 0))
        mark(("sqrt", 0), act(DV0[0:96, 41:44], DV0[0:96, 38:41], ACT.Sqrt))
        wait(DV, ("sqrt", 0))
        mark(("rsqrt", 0), DV.inc(v.reciprocal(DV0[0:96, 38:41], DV0[0:96, 41:44])))
        wait(DV, ("rsqrt", 0))
        for i in range(3):
            tt(DV0[0:96, 32 + i:33 + i], DV0[0:96, 38 + i:39 + i], vec(f"bn{i + 1}", 0), MUL)
        v.tensor_scalar(DV0[0:96, 44:45], vec("bn1", 2), -1.0, None, MUL)
        for i in (1, 2):
            mark(("b-m", 0), tt(DV0[0:96, 44 + i:45 + i], vec(f"c{i}b"), vec(f"bn{i + 1}", 2), SUB))
        wait(DV, ("b-m", 0))
        for i in range(3):
            stt(DV0[0:96, 35 + i:36 + i], DV0[0:96, 44 + i:45 + i], DV0[0:96, 32 + i:33 + i],
                vec(f"bn{i + 1}", 1), MUL, ADD)

    def borders(img, n, P):
        for y in (0, PADW - 1):
            nc.vector.memset(img[0:P, 0:n, y, :], 0.0)
        for x in (0, PADW - 1):
            t = DV.inc(nc.vector.memset(img[0:P, 0:n, 1:PADW - 1, x], 0.0))
        return t

    def conv9(key, o, P, wt, img, i, taps=range(9)):
        for tap in taps:
            dy, dx = divmod(tap, 3)
            t = mm(o[0:P, :], wt(tap), img[:, 8 * i + dy:8 * i + dy + 8, dx:dx + 64], tap == taps[0], tap == taps[-1])
            if tap == taps[-1]:
                mark(key, PE.inc(t))
            yield 0.86

    def tap_rows(img, i, tap):
        dy, dx = divmod(tap, 3)
        return img[:, 8 * i + dy:8 * i + dy + 8, dx:dx + 64]

    def side_taps(key, m, P, img, w, bias, i, ready):
        o = T1[0:P, m % 3, :]
        o8 = PX[0:P, (m % 3) * 512:(m % 3 + 1) * 512]
        wait(AC, ready, (key + "silu", m - 3))
        act(o.rearrange("p (y x) -> p y x", y=8), tap_rows(img, i, 7), ACT.Identity, bias=bias, scale=WH[0:P, w + 7:w + 8])
        mark((key + "taps78", m), act(o8.rearrange("p (y x) -> p y x", y=8), tap_rows(img, i, 8), ACT.Copy,
                                      scale=WH[0:P, w + 8:w + 9]))
        wait(PO, (key + "taps78", m))
        mark((key + "side", m), ptt(o, o, o8, ADD))

    def merge_taps(key, m, P, n, pb, img, w, i):
        x = T1[0:P, m % 3, :]
        wait(DV, (key + "conv", m), (key + "side", m))
        x3 = x.rearrange("p (y x) -> p y x", y=8)
        for tap in range(NTAP, 7):
            mark((key + "tap", m), stt(x3, tap_rows(img, i, tap), WH[0:P, w + tap:w + tap + 1], x3, MUL, ADD))
            wait(DV, (key + "tap", m))
        mark((key + "half", m), tt(x, x, pb[0:P, :], ADD))
        emptied(n, done[key + "half", m])
        wait(AC, (key + "half", m), (key + "silu", m - 3))
        mark((key + "tanh", m), act(T0[0:P, m % 3, :], x, ACT.Tanh))

    def layer0(b, par):
        phase()
        ra, rb = Cutter(RA, 3 * PADN), Cutter(RB, 2 * L)
        XP = ra(3 * PADN).rearrange("p (j y x) -> p j y x", j=3, y=PADW)
        wx = rb(768, 96).rearrange("p (k c) -> p k c", k=2)
        DG = rb(27 * 128).rearrange("p (t c) -> p t c", t=27)
        wxp = rb(420).rearrange("p (j c) -> p j c", j=3)
        XJ = [rb(512) for _ in range(3)]
        TK = [rb(524) for _ in range(2)]
        PRK = rb(384)
        dma(("a.wx", 0), "w0", wx, A["win"][:, :, 0:384])
        dma(("a.wxp", 0), "w1", wxp, A["wxp0"])
        for i in range(27):
            mark(("a.diag", 0), PO.inc(nc.gpsimd.tensor_scalar(DG[:, i, :], IDENT, WH[:, i:i + 1], 1.0, MUL, MUL)))
        mark(("a.rim", 0), borders(XP, 3, 128))
        yield 2
        xv = A["x"][b].rearrange("(i q p) c -> i p q c", q=4, p=128)

        def load(i):
            wait(SP, ("a.xT", 2 * (i - 2) + 1))
            dma(("a.x", i), f"xi{i % 2}", XI[:, i % 2, :, :], xv[i])
            yield 0

        def turn(i):
            wait(PE, ("a.x", i))
            for hh in range(2):
                n, pb = bank()
                for q in range(4):
                    t = nc.tensor.transpose(pb[0:96, q * 128:(q + 1) * 128],
                                            XI[:, i % 2, q, hh * 96:(hh + 1) * 96], IDENT)
                mark(("a.xT", 2 * i + hh), PE.inc(t))
                wait(AC, ("a.xT", 2 * i + hh), ("a.proj", i - 2), ("a.xTout", i - 2))
                emptied(n, act(XT[:, i % 2, hh, :], pb[0:96, :], ACT.Copy))
            mark(("a.xTc", i), done["emptied", n])
            yield 1
            wait(SP, ("a.xTc", i))
            dma(("a.xTout", i), f"xt{i % 2}", xTd[:, :, i * 512:(i + 1) * 512].rearrange("k p n -> p k n"),
                XT[:, i % 2, :, :])

        def project(i):
            wait(PE, ("a.wx", 0), ("a.xTc", i))
            for j in range(3):
                n, pb = bank()
                for k in range(2):
                    t = mm(pb[:, :], wx[:, k, j * 128:(j + 1) * 128], XT[:, i % 2, k, :], k == 0, k == 1)
                mark(("a.proj", i), PE.inc(t))
                wait(AC, ("a.proj", i))
                emptied(n, act(XP[:, j, 1 + 8 * i:9 + 8 * i, 1:65], pb[:, :].rearrange("p (y x) -> p y x", y=8),
                               ACT.Copy))
                yield 1.7
            mark(("a.rows", i), done["emptied", n])
        yield from woven(8, load, turn, project)

        tkv = tkd.rearrange("(i p) c -> i p c", p=128)
        for eng in (PE, AC, DV):
            wait(eng, ("a.diag", 0), ("a.rim", 0))

        def side(m):
            i, j = divmod(m, 3)
            side_taps("a.", m, 128, XP[:, j], 9 * j, DV0[:, 15 + j:16 + j], i, ("a.rows", min(i + 1, 7)))
            yield 0

        def conv(m):
            i, j = divmod(m, 3)
            wait(PE, ("a.rows", min(i + 1, 7)))
            wait(DV, ("a.rows", min(i + 1, 7)))
            n, pb = bank()
            yield from conv9(("a.conv", m), pb, 128, lambda tap: DG[:, j * 9 + tap, :], XP[:, j], i, range(NTAP))
            merge_taps("a.", m, 128, n, pb, XP[:, j], 9 * j, i)

        def silu(m):
            i, j = divmod(m, 3)
            wait(DV, ("a.tanh", m), ("a.tproj", 4 * (i - 1) + 3), ("a.xcout", m - 3))
            mark(("a.silu", m), stt(XJ[j], T0[:, m % 3, :], 1.0, T1[:, m % 3, :], ADD, MUL))
            yield 0
            wait(SP, ("a.silu", m))
            dma(("a.xcout", m), f"xj{j}", xc0[j, :, i * 512:(i + 1) * 512], XJ[j])
            if j < 2:
                return
            for q in range(4):
                c = 4 * i + q
                qs = slice(q * 128, (q + 1) * 128)
                wait(PE, ("a.silu", m))
                n, pb = bank()
                for j_ in range(3):
                    t = nc.tensor.transpose(pb[:, j_ * 128:(j_ + 1) * 128], XJ[j_][:, qs], IDENT)
                mark(("a.tturn", c), PE.inc(t))
                n2, pb2 = bank()
                for j_ in range(3):
                    t = mm(pb2[:, 0:140], XJ[j_][:, qs], wxp[:, j_, :], j_ == 0, j_ == 2)
                mark(("a.tproj", c), PE.inc(t))
                tk = TK[c % 2]
                wait(AC, ("a.tproj", c), ("a.tkout", c - 2))
                emptied(n, act(tk[:, 70:454], pb[:, 0:384], ACT.Copy))
                act(tk[:, 0:70], pb2[:, 0:70], ACT.Copy)
                act(tk[:, 454:524], pb2[:, 70:140], ACT.Copy)
                emptied(n2, act(PRK[:, c * 12:c * 12 + 12].rearrange("p (k h) -> p k h", k=2),
                                pb2[:, 0:140].rearrange("p (k c) -> p k c", k=2)[:, :, 64:70], ACT.Copy))
                yield 1.8
                wait(SP, ("emptied", n2))
                dma(("a.tkout", c), f"tk{c % 2}", tkv[c], tk)
        wait(PE, ("a.wxp", 0))
        yield from pipeline(24, side, idle, conv, silu)

        a = VCOL["dtb0"][0]
        wait(DV, ("emptied", bank_no[0] - 1))
        tt(PRK.rearrange("p (c h) -> p c h", c=32), PRK.rearrange("p (c h) -> p c h", c=32),
           V[:, a:a + 12].unsqueeze(1).to_broadcast([128, 32, 12]), ADD)
        phase()
        ra = Cutter(RA, 3 * PADN)
        S0, S1, S2, DT, AT, ES = (ra(384) for _ in range(6))
        DTT = ra(768).rearrange("p (u w h) -> p u w h", u=64, w=2)
        SB_ = ra(576).bitcast(BF).rearrange("p (a n) -> p a n", a=3)
        HS = ra(768, 32)
        rb2 = Cutter(RB, 2 * L)
        RL = [rb2(1536, 96).bitcast(BF).rearrange("p (a n) -> p a n", a=2) for _ in range(2)]
        for rl in RL:
            mark(("b.zero", 0), DV.inc(nc.vector.memset(rl, 0.0)))
        wait(DV, ("b.zero", 0))
        for rl in RL:
            nc.vector.memset(rl[32:64, 0, :], -1.0)
            mark(("b.rows", 0), DV.inc(nc.vector.memset(rl[0:32, 1, :], 1.0)))
        mark(("b.abs", 0), act(S1, PRK, ACT.Abs))
        wait(AC, ("b.abs", 0))
        mark(("b.exp", 0), act(S1, S1, ACT.Exp, scale=-1.0))
        wait(AC, ("b.exp", 0))
        mark(("b.ln", 0), act(S1, S1, ACT.Ln, bias=ONE[:, 0:1]))
        wait(DV, ("b.ln", 0))
        mark(("b.steps", 0), stt(S0, PRK, 0.0, S1, MAX, ADD))
        wait(SP, ("b.steps", 0))
        dma(("b.dtout", 0), "w0", dtd.rearrange("(c p) h -> p c h", p=128), S0.rearrange("p (c h) -> p c h", c=32))
        dtv = DT.rearrange("p (c k h) -> p c k h", c=32, k=2)
        wait(DV, ("b.steps", 0))
        mark(("b.dt0", 0), DV.inc(nc.vector.tensor_copy(
            dtv[:, :, 0, :], S0.rearrange("p (c k h) -> p c k h", c=32, k=2)[:, :, 0, :])))
        dcol = dtd.rearrange("(h c w) n -> w h c n", h=64, w=2)
        wait(SP, ("b.dtout", 0))
        for w in range(2):
            dma(("b.dt1", 0), "w1", dtv[64 * w:64 * w + 64, :, 1, :], dcol[w][:, :, 6:12])
        yield 18 * W_CHAIN
        wait(DV, ("b.dt0", 0), ("b.dt1", 0), ("b.dtout", 0))
        mark(("b.la", 0), tt(S0.rearrange("p (c h) -> p c h", c=32), DT.rearrange("p (c h) -> p c h", c=32),
                             DV0[:, 0:12].unsqueeze(1).to_broadcast([128, 32, 12]), MUL))
        (n1, p1), (n2, p2) = bank(), bank()
        wait(PE, ("b.la", 0))
        mm(p1[:, 0:384], TRI, S0, True, True)
        mark(("b.sums", 0), PE.inc(mm(p2[:, 0:384], ONES, S0, True, True)))
        wait(DV, ("b.sums", 0))
        mark(("b.cum", 0), DV.inc(nc.vector.tensor_copy(S1, p1[:, 0:384])))
        emptied(n1, done["b.cum", 0])
        wait(DV, ("b.cum", 0))
        mark(("b.left", 0), tt(S2, p2[:, 0:384], S1, SUB))
        wait(AC, ("b.left", 0))
        emptied(n2, act(AT, p2[:, 0:384], ACT.Exp))
        mark(("b.w", 0), act(S2, S2, ACT.Exp))
        mark(("b.es", 0), act(ES, S1, ACT.Exp))
        yield 8 * W_CHAIN
        d3 = DT.rearrange("p (u h) -> p u h", u=64)
        mark(("b.dtt0", 0), DV.inc(nc.vector.tensor_copy(DTT[:, :, 0, :], d3)))
        wait(DV, ("b.w", 0))
        mark(("b.dtt", 0), tt(DTT[:, :, 1, :], d3, S2.rearrange("p (u h) -> p u h", u=64), MUL))
        n, pb = bank()
        wait(PE, ("b.cum", 0))
        for j in range(3):
            t = nc.tensor.transpose(pb[:, j * 128:(j + 1) * 128], S1[:, j * 128:(j + 1) * 128], IDENT)
        mark(("b.rowT", 0), PE.inc(t))
        wait(DV, ("b.rowT", 0))
        mark(("b.part0", 0), DV.inc(nc.vector.tensor_copy(SB_[:, 0, :], pb[:, 0:384])))
        wait(DV, ("b.part0", 0))
        mark(("b.rest1", 0), tt(S0, pb[:, 0:384], SB_[:, 0, :], SUB))
        emptied(n, done["b.rest1", 0])
        wait(DV, ("b.rest1", 0))
        mark(("b.part1", 0), DV.inc(nc.vector.tensor_copy(SB_[:, 1, :], S0)))
        wait(DV, ("b.part1", 0))
        mark(("b.parts", 0), tt(SB_[:, 2, :], S0, SB_[:, 1, :], SUB))
        wait(SP, ("b.parts", 0))
        for i in range(3):
            dma(("b.spout", 0), "w2", spd[i].rearrange("(j q) t -> q j t", q=128),
                SB_[:, i, :].rearrange("p (j t) -> p j t", j=3))
        dma(("b.state", -1), "w3", HS, A["h0"])
        done["b.state0", -1] = done["b.state1", -1] = done["b.state", -1]
        yield 12 * W_CHAIN
        TK = [ra(454) for _ in range(5)]
        CC = [ra(256, 32) for _ in range(3)]
        DX = [ra(768) for _ in range(2)] + [rb2(768)]
        EE = [ra(768) for _ in range(2)]
        MM = [rb2(768) for _ in range(2)]
        YO = [ra(384) for _ in range(4)]
        tkc = tkd.rearrange("(h c w) n -> c w h n", h=64, w=2)
        ycol = y0d[1].rearrange("(h c w) n -> c w h n", h=64, w=2)
        wait(PE, ("b.rows", 0))

        def fetch(u):
            c, k = divmod(u, 2)
            if k == 0:
                wait(SP, ("b.decay", u - 3), ("b.spout", 0))
                src = spd[:, c * 12:c * 12 + 12, :].rearrange("a h t -> a (h t)")
                dma(("b.rl", c), f"rl{c % 2}", RL[c % 2][0:3, 0, :], src)
                dma(("b.rl", c), f"rl{c % 2}", RL[c % 2][32:35, 1, :], src)
            wait(SP, ("b.upd", u - 5), ("b.dx", u - 5))
            tk = TK[u % 5]
            if k == 0:
                dma(("b.tk", u), f"tk{u % 5}", tk, tkd[c * 128:(c + 1) * 128, 0:454])
            else:
                dma(("b.tk", u), f"tk{u % 5}", tk, tkc[c][:, :, 70:524])
            yield 0

        def prepare(u):
            c, k = divmod(u, 2)
            tk, xo, po = TK[u % 5], (70, 0)[k], (0, 384)[k]
            cc, dx, ee = CC[u % 3], DX[u % 3], EE[u % 2]
            wait(PE, ("b.tk", u))
            n, pb = bank()
            nc.tensor.transpose(pb[0:32, 0:128], tk[:, po:po + 32], IDENT)
            mark(("b.cbT", u), PE.inc(nc.tensor.transpose(pb[0:32, 128:256], tk[:, po + 32:po + 64], IDENT)))
            wait(AC, ("b.cbT", u), ("b.carry", u - 3))
            mark(("b.cb", u), act(cc, pb[0:32, 0:256], ACT.Copy))
            emptied(n, done["b.cb", u])
            wait(PO, ("b.tk", u), ("b.dtt0", 0), ("b.dtt", 0), ("b.y", u - 3))
            mark(("b.dx", u), ptt(
                dx.rearrange("p (w h q) -> p w h q", w=2, h=6),
                tk[:, xo:xo + 384].rearrange("p (h q) -> p h q", h=6).unsqueeze(1).to_broadcast([128, 2, 6, 64]),
                DTT[:, u, :, :].unsqueeze(3).to_broadcast([128, 2, 6, 64]), MUL))
            wait(PE, ("b.rl", c))
            for hf in range(2):
                n, pb = bank()
                for h in range(3):
                    q = (k * 6 + hf * 3 + h) * 128
                    mm(pb[:, h * 128:(h + 1) * 128], RL[c % 2][:, 1, q:q + 128], RL[c % 2][:, 0, q:q + 128],
                       h == 0, False)
                t = mm(pb[:, 0:384].rearrange("p (h t) -> p h t", h=3), IDB[:, :],
                       NEGB[:, :].unsqueeze(1).to_broadcast([128, 3, 128]), False, True)
                mark(("b.decay", u), PE.inc(t))
                wait(AC, ("b.decay", u), ("b.mix", u - 2))
                emptied(n, act(ee[:, hf * 384:(hf + 1) * 384], pb[:, 0:384], ACT.Exp))
                yield 0.7
            mark(("b.exp", u), done["emptied", n])

        def mix(u):
            cc, ee, mx = CC[u % 3], EE[u % 2], MM[u % 2]
            n, pb = bank()
            wait(PE, ("b.cb", u))
            mark(("b.g", u), PE.inc(mm(pb[:, 0:128], cc[:, 128:256], cc[:, 0:128], True, True)))
            wait(DV, ("b.exp", u), ("b.g", u), ("b.y", u - 2))
            mark(("b.mix", u), tt(mx.rearrange("p (h t) -> p h t", h=6), ee.rearrange("p (h t) -> p h t", h=6),
                                  pb[:, 0:128].unsqueeze(1).to_broadcast([128, 6, 128]), MUL))
            emptied(n, done["b.mix", u])
            yield 0.5

        def out(u):
            c, k = divmod(u, 2)
            tk, xo, po = TK[u % 5], (70, 0)[k], (0, 384)[k]
            cc, dx, mx, yo = CC[u % 3], DX[u % 3], MM[u % 2], YO[u % 4]
            hv = HS[:, k * 384:(k + 1) * 384]
            n, pc = bank()
            wait(PE, ("b.cb", u), (f"b.state{k}", u - 2) if u > 1 else ("b.state", -1))
            mark(("b.carry", u), PE.inc(mm(pc[:, 0:384], cc[:, 0:128], hv, True, True)))
            wait(DV, ("b.carry", u), ("b.es", 0))
            mark(("b.fade", u), tt(
                hv.rearrange("p (h q) -> p h q", h=6), hv.rearrange("p (h q) -> p h q", h=6),
                AT[0:32, u * 6:u * 6 + 6].unsqueeze(2).to_broadcast([32, 6, 64]), MUL))
            wait(DV, ("b.yout", u - 4))
            mark(("b.ycarry", u), tt(
                yo.rearrange("p (h q) -> p h q", h=6), pc[:, 0:384].rearrange("p (h q) -> p h q", h=6),
                ES[:, u * 6:u * 6 + 6].unsqueeze(2).to_broadcast([128, 6, 64]), MUL))
            emptied(n, done["b.ycarry", u])
            n, pst = bank()
            wait(PE, ("b.dx", u))
            mark(("b.upd", u), PE.inc(mm(pst[0:32, 0:384], tk[:, po + 32:po + 64], dx[:, 384:768], True, True)))
            wait(DV, ("b.upd", u), ("b.fade", u))
            mark((f"b.state{k}", u), tt(hv, hv, pst[0:32, 0:384], ADD))
            emptied(n, done[f"b.state{k}", u])
            yield 1.2
            n, py = bank()
            wait(PE, ("b.mix", u))
            for h in range(6):
                t = mm(py[:, h * 64:(h + 1) * 64], mx[:, h * 128:(h + 1) * 128], dx[:, h * 64:(h + 1) * 64], True, True)
            mark(("b.y", u), PE.inc(t))
            wait(DV, ("b.y", u), ("b.ycarry", u))
            mark(("b.ysum", u), tt(yo, yo, py[:, 0:384], ADD))
            emptied(n, done["b.ysum", u])
            yield 0.8

        def store(u):
            c, k = divmod(u, 2)
            wait(SP, ("b.ysum", u))
            if k == 0:
                dma(("b.yout", u), f"yo{u % 4}", y0d[0, c * 128:(c + 1) * 128, :], YO[u % 4])
            else:
                dma(("b.yout", u), f"yo{u % 4}", ycol[c], YO[u % 4])
            yield 0
        yield from scaled(W_SSD, woven(64, fetch, idle, prepare, mix, out, store))

        phase()
        ra, rb = Cutter(RA, 3 * PADN), Cutter(RB, 2 * L)
        HB = [[ra(512) for _ in range(6)], [PX[:, j * 512:(j + 1) * 512] for j in range(6)]]
        YG = [ra(512) for _ in range(3)]
        XO = [ra(1024, 96) for _ in range(2)] + [B2[:, :, :].rearrange("p a n -> p (a n)")]
        XS = [ra(1024, 96), X2[:, :, :].rearrange("p a n -> p (a n)")]
        Y0, Y1 = ra(1536), ra(1536)
        wz = rb(768, 96).rearrange("p (k c) -> p k c", k=2)
        wo = rb(576).rearrange("p (j c) -> p j c", j=3)
        w1 = rb(1536, 96).rearrange("p (k c) -> p k c", k=2)
        w2 = rb(1152).rearrange("p (j c) -> p j c", j=6)
        XCR = [rb(1536) for _ in range(2)]
        dma(("c.w", 0), "w0", wz, A["win"][:, :, 384:768])
        dma(("c.w", 0), "w0", wo, A["wout0"])
        dma(("c.w", 0), "w0", w1, A["w1"])
        dma(("c.w", 0), "w0", w2, A["w2"])
        yield 5 * W_CHAIN
        yv = y0d.rearrange("k (i q p) c -> k i p q c", q=4, p=128)

        def cload(i):
            cs_ = slice(i * 512, (i + 1) * 512)
            wait(SP, ("c.xo", i - 2), ("c.yT", 3 * (i - 1) + 2), ("c.ysum", i - 1), ("c.yr", 3 * (i - 2) + 2))
            dma(("c.y0", i), "y0", Y0.rearrange("p (q c) -> p q c", q=4), yv[0, i])
            dma(("c.y1", i), "y1", Y1.rearrange("p (q c) -> p q c", q=4), yv[1, i])
            dma(("c.xT", i), f"xt{i % 2}", XT[:, i % 2, :, :], xTd[:, :, cs_].rearrange("k p n -> p k n"))
            dma(("c.xc", i), f"xc{i % 2}", XCR[i % 2].rearrange("p (j n) -> p j n", j=3),
                xc0[:, :, cs_].rearrange("j p n -> p j n"))
            yield 0

        def gate(i):
            wait(PO, ("c.y0", i), ("c.y1", i))
            mark(("c.ysum", i), ptt(Y0, Y0, Y1, ADD))
            wait(PE, ("c.xT", i), ("c.w", 0))
            for j in range(3):
                m = 3 * i + j
                n, pb = bank()
                for k in range(2):
                    t = mm(pb[:, :], wz[:, k, j * 128:(j + 1) * 128], XT[:, i % 2, k, :], k == 0, k == 1)
                mark(("c.z", m), PE.inc(t))
                wait(AC, ("c.z", m), ("c.yg", m - 3))
                mark(("c.tanh", m), act(T0[:, m % 3, :], pb[:, :], ACT.Tanh, scale=0.5))
                wait(DV, ("c.tanh", m))
                mark(("c.silu", m), stt(T0[:, m % 3, :], T0[:, m % 3, :], 1.0, pb[:, :], ADD, MUL))
                emptied(n, done["c.silu", m])
                yield 1.7
                n, pb = bank()
                wait(PE, ("c.ysum", i))
                for q in range(4):
                    t = nc.tensor.transpose(pb[:, q * 128:(q + 1) * 128],
                                            Y0[:, q * 384 + j * 128:q * 384 + (j + 1) * 128], IDENT)
                mark(("c.yT", m), PE.inc(t))
                wait(DV, ("c.yT", m), ("c.xc", i))
                mark(("c.yr", m), stt(T1[:, m % 3, :], XCR[i % 2][:, j * 512:(j + 1) * 512], DV0[:, 12 + j:13 + j],
                                      pb[:, :], MUL, ADD))
                emptied(n, done["c.yr", m])
                wait(DV, ("c.silu", m), ("c.yr", m), ("c.out", i - 1))
                mark(("c.yg", m), stt(YG[j], T0[:, m % 3, :], 0.5, T1[:, m % 3, :], MUL, MUL))
                yield 0.5

        def outp(i):
            xo = XO[i % 3]
            wait(PE, ("c.yg", 3 * i + 2))
            for m in range(2):
                n, pb = bank()
                for j in range(3):
                    t = mm(pb[0:96, :], wo[:, j, m * 96:(m + 1) * 96], YG[j], j == 0, j == 2)
                mark(("c.out", i), PE.inc(t))
                wait(DV, ("c.out", i), ("c.x1", i - 3), ("c.xT", i))
                mark(("c.xo", i), tt(xo[:, m * 512:(m + 1) * 512], pb[0:96, :], XT[:, i % 2, m, :], ADD))
                emptied(n, done["c.xo", i])
                yield 2.6

        def mlp(i):
            xo = XO[i % 3]
            wait(PE, ("c.xo", i))
            for j in range(6):
                m = 6 * i + j
                n, pb = bank()
                for k in range(2):
                    t = mm(pb[:, :], w1[:, k, j * 128:(j + 1) * 128], xo[:, k * 512:(k + 1) * 512], k == 0, k == 1)
                mark(("c.h", m), PE.inc(t))
                ta, tb = MA[m % 2], MB[m % 2]
                wait(AC, ("c.h", m), ("c.hs", m - 2))
                act(ta, pb[:, :], ACT.Tanh, bias=DV0[:, 18 + j:19 + j], scale=0.5)
                emptied(n, act(tb, pb[:, :], ACT.Identity, bias=DV0[:, 18 + j:19 + j], scale=0.5))
                wait(DV, ("emptied", n), ("c.mlp", i - 2))
                mark(("c.hs", m), stt(HB[i % 2][j], ta, 1.0, tb, ADD, MUL))
                yield 1.7

        def mlp2(i):
            xo, xs = XO[i % 3], XS[i % 2]
            cs_ = slice(i * 512, (i + 1) * 512)
            wait(PE, ("c.hs", 6 * i + 5))
            for m in range(2):
                n, pb = bank()
                for j in range(6):
                    t = mm(pb[0:96, :], w2[:, j, m * 96:(m + 1) * 96], HB[i % 2][j], j == 0, j == 5)
                    if j == 2:
                        yield 2.5
                mark(("c.mlp", i), PE.inc(t))
                wait(DV, ("c.mlp", i), ("c.x1out", i - 2))
                mark(("c.x1", i), stt(xs[:, m * 512:(m + 1) * 512], pb[0:96, :], vec("b2", m),
                                      xo[:, m * 512:(m + 1) * 512], ADD, ADD))
                emptied(n, done["c.x1", i])
                yield 2.6
            wait(SP, ("c.x1", i))
            dma(("c.x1out", i), f"xs{i % 2}", x1d[par, :, :, cs_].rearrange("k p n -> p k n"),
                xs.rearrange("p (k n) -> p k n", k=2))
        MA, MB = [XI[:, i, :, :].rearrange("p a c -> p (a c)")[:, 0:512] for i in range(2)], [rb(512), ra(512)]
        yield from woven(8, cload, gate, outp, mlp, mlp2)

    def layer1(b, par):
        phase()
        ra, rb = Cutter(RA, 3 * PADN), Cutter(RB, 2 * L)
        YP = ra(2 * PADN, 96).rearrange("p (j y x) -> p j y x", j=2, y=PADW)
        c1 = rb(864, 96).rearrange("p (t c) -> p t c", t=9)
        c2 = rb(864, 96).rearrange("p (t c) -> p t c", t=9)
        c3 = rb(96, 96)
        dma(("d.w", 0), "w0", c1, A["c1"])
        dma(("d.w", 0), "w0", c2, A["c2"])
        dma(("d.w", 0), "w0", c3, A["c3"])
        yield 5 * W_CHAIN
        mark(("d.rim", 0), borders(YP, 2, 96))
        wait(AC, ("d.rim", 0))
        for i in range(8):
            wait(SP, ("d.in", i - 2))
            dma(("d.x", i), f"xt{i % 2}", XT[:, i % 2, 0, :], x1d[par, 0, :, i * 512:(i + 1) * 512])
            wait(AC, ("d.x", i))
            mark(("d.in", i), act(YP[:, 0, 1 + 8 * i:9 + 8 * i, 1:65],
                                  XT[:, i % 2, 0, :].rearrange("p (y x) -> p y x", y=8), ACT.Identity,
                                  bias=DV0[0:96, 35:36], scale=DV0[0:96, 32:33]))
            yield 0.5
        wait(PE, ("d.w", 0))

        def conv1(i):
            wait(PE, ("d.in", min(i + 1, 7)))
            n, pb = bank()
            yield from conv9(("d.c1", i), pb, 96, lambda tap: c1[:, tap, :], YP[:, 0], i)
            wait(AC, ("d.c1", i))
            mark(("d.y1", i), act(YP[:, 1, 1 + 8 * i:9 + 8 * i, 1:65], pb[0:96, :].rearrange("p (y x) -> p y x", y=8),
                                  ACT.Relu, bias=DV0[0:96, 36:37], scale=DV0[0:96, 33:34]))
            emptied(n, done["d.y1", i])

        def conv2(i):
            wait(PE, ("d.y1", min(i + 1, 7)))
            n, pb = bank()
            yield from conv9(("d.c2", i), pb, 96, lambda tap: c2[:, tap, :], YP[:, 1], i)
            wait(AC, ("d.c2", i), ("d.c3", i - 3))
            mark(("d.y2", i), act(T0[0:96, i % 3, :], pb[0:96, :], ACT.Relu, bias=DV0[0:96, 37:38],
                                  scale=DV0[0:96, 34:35]))
            emptied(n, done["d.y2", i])

        def conv3(i):
            n, pb = bank()
            wait(PE, ("d.y2", i))
            mark(("d.c3", i), PE.inc(mm(pb[0:96, :], c3, T0[0:96, i % 3, :], True, True)))
            wait(AC, ("d.c3", i), ("d.xlout", i - 3))
            mark(("d.xl", i), act(T1[0:96, i % 3, :], pb[0:96, :], ACT.Relu, bias=vec("c3b")))
            emptied(n, done["d.xl", i])
            yield 0.9
            wait(SP, ("d.xl", i))
            dma(("d.xlout", i), f"t1{i % 3}", xld[par, :, i * 512:(i + 1) * 512], T1[0:96, i % 3, :])
        yield from pipeline(8, conv1, idle, conv2, conv3)
        phase()
        ra, rb = Cutter(RA, 3 * PADN), Cutter(RB, 2 * L)
        YP = ra(2 * PADN, 96).rearrange("p (j y x) -> p j y x", j=2, y=PADW)
        wip, wig = ra(384, 96), ra(384, 96)
        DG = ra(18 * 96, 96).rearrange("p (t c) -> p t c", t=18)
        ZT, ZO = [ra(512, 96) for _ in range(2)], [XI[0:96, i, :, :].rearrange("p a c -> p (a c)")[:, 0:512] for i in range(2)]
        XM, VR = rb(L, 96), rb(L, 96)
        dma(("e.w", 0), "w0", wip, A["wip"])
        yield 5 * W_CHAIN
        wait(DV, ("e.w", 0))
        mark(("e.wg", 0), DV.inc(nc.vector.tensor_scalar(wig, wip, vec("lng"), None, MUL)))
        n, pb = bank()
        wait(PE, ("e.w", 0))
        for e in range(4):
            t = mm(pb[0:96, e:e + 1], wip[:, e * 96:(e + 1) * 96], vec("lnb"), True, True)
        mark(("e.b", 0), PE.inc(t))
        ipb, ipc = IPW[:, 0:4], IPW[:, 4:8]
        wait(AC, ("e.b", 0))
        mark(("e.ipb", 0), act(ipb, pb[0:96, 0:4], ACT.Copy))
        emptied(n, act(ipc, pb[0:96, 0:4], ACT.Copy, scale=0.5))
        mark(("e.ipc", 0), done["emptied", n])
        for i in range(18):
            mark(("e.diag", 0), PO.inc(nc.gpsimd.tensor_scalar(DG[:, i, :], IDENT[0:96, 0:96],
                                                               WH[0:96, 27 + i:28 + i], 1.0, MUL, MUL)))
        mark(("e.rim", 0), borders(YP, 2, 96))
        yield 1

        def nload(i):
            wait(SP, ("e.xm", i - 2))
            dma(("e.x", i), f"xt{i % 2}", XT[:, i % 2, 0, :], x1d[par, 1, :, i * 512:(i + 1) * 512])
            yield 0

        def mean(i):
            cs_ = slice(i * 512, (i + 1) * 512)
            n, pb = bank()
            wait(PE, ("e.x", i))
            mark(("e.mean", i), PE.inc(mm(pb[0:96, :], M96[:, :], XT[:, i % 2, 0, :], True, True)))
            wait(DV, ("e.mean", i))
            mark(("e.xm", i), tt(XM[:, cs_], XT[:, i % 2, 0, :], pb[0:96, :], SUB))
            emptied(n, done["e.xm", i])
            wait(AC, ("e.xm", i), ("e.var", i - 3))
            mark(("e.sq", i), act(T0[0:96, i % 3, :], XM[:, cs_], ACT.Square))
            yield 0.9

        def var(i):
            cs_ = slice(i * 512, (i + 1) * 512)
            n, pb = bank()
            wait(PE, ("e.sq", i))
            mark(("e.var", i), PE.inc(mm(pb[0:96, :], M96[:, :], T0[0:96, i % 3, :], True, True)))
            wait(AC, ("e.var", i))
            mark(("e.vr", i), act(VR[:, cs_], pb[0:96, :], ACT.Copy))
            emptied(n, done["e.vr", i])
            yield 0.9
        yield from woven(8, nload, mean, var)
        wait(AC, ("e.vr", 7))
        mark(("e.ln", 0), act(VR, VR, ACT.Ln, bias=ONE[0:96, 1:2]))
        yield 6 * W_CHAIN
        wait(AC, ("e.ln", 0))
        mark(("e.rstd", 0), act(VR, VR, ACT.Exp, scale=-0.5))
        yield 6 * W_CHAIN
        wait(DV, ("e.rstd", 0), ("e.xm", 7))
        wait(PE, ("e.wg", 0), ("e.diag", 0), ("e.rim", 0))
        wait(AC, ("e.ipb", 0), ("e.ipc", 0), ("e.rim", 0))

        def norm(i):
            cs_ = slice(i * 512, (i + 1) * 512)
            wait(DV, ("e.p", 4 * (i - 3) + 3))
            mark(("e.xn", i), tt(T0[0:96, i % 3, :], XM[:, cs_], VR[:, cs_], MUL))
            yield 0

        def inproj(i):
            cs_ = slice(i * 512, (i + 1) * 512)
            wait(PE, ("e.xn", i))
            for e in range(4):
                n, pb = bank()
                mark(("e.p", 4 * i + e), PE.inc(mm(pb[0:96, :], wig[:, e * 96:(e + 1) * 96], T0[0:96, i % 3, :], True, True)))
                if e < 2:
                    wait(AC, ("e.p", 4 * i + e))
                    emptied(n, act(YP[:, e, 1 + 8 * i:9 + 8 * i, 1:65], pb[0:96, :].rearrange("p (y x) -> p y x", y=8),
                                   ACT.Identity, bias=ipb[:, e:e + 1]))
                    mark(("e.rows", i), done["emptied", n])
                else:
                    m = 2 * i + e - 2
                    s_ = m % 2
                    wait(AC, ("e.p", 4 * i + e), ("e.z", m - 2), ("e.zout", m - 2))
                    act(ZT[s_], pb[0:96, :], ACT.Tanh, bias=ipc[:, e:e + 1], scale=0.5)
                    emptied(n, act(ZO[s_], pb[0:96, :], ACT.Identity, bias=ipc[:, e:e + 1], scale=0.5))
                    wait(DV, ("emptied", n))
                    mark(("e.z", m), stt(ZO[s_], ZT[s_], 1.0, ZO[s_], ADD, MUL))
                    wait(SP, ("e.z", m))
                    dma(("e.zout", m), f"xi{s_}", zd[par, e - 2, :, cs_], ZO[s_])
                yield 0.9
        yield from woven(8, idle, norm, inproj)
        C1 = RB[0:96, 0:2 * L].rearrange("p (j l) -> p j l", j=2)
        C1T = RB[0:96, 0:2 * L].rearrange("p (j h w) -> p j w h", j=2, h=64)
        wait(DV, ("e.xn", 7), ("e.rows", 7))
        wait(DV, ("e.rim", 0))

        def side(m):
            j, i = divmod(m, 8)
            side_taps("e.", m, 96, YP[:, j], 27 + 9 * j, DV0[0:96, 24 + j:25 + j], i, ("e.rows", min(i + 1, 7)))
            yield 0

        def dconv(m):
            j, i = divmod(m, 8)
            wait(PE, ("e.rows", min(i + 1, 7)))
            n, pb = bank()
            yield from conv9(("e.conv", m), pb, 96, lambda tap: DG[:, j * 9 + tap, :], YP[:, j], i, range(NTAP))
            wait(AC, ("e.p", 31))
            merge_taps("e.", m, 96, n, pb, YP[:, j], 27 + 9 * j, i)

        def silu(m):
            j, i = divmod(m, 8)
            wait(DV, ("e.tanh", m))
            mark(("e.silu", m), stt(C1[:, j, i * 512:(i + 1) * 512], T0[0:96, m % 3, :], 1.0, T1[0:96, m % 3, :], ADD, MUL))
            yield 0
        yield from pipeline(16, side, idle, dconv, silu)
        phase()
        ra = Cutter(RA, 3 * PADN)
        HW_ = 1024
        flat = [t[0:96].rearrange("p a n -> p (a n)")[:, 0:HW_] for t in (T0, T1, B2, X2)] + \
            [XT[:, i, :, :].rearrange("p a n -> p (a n)") for i in range(2)]
        bufs = flat + [ra(HW_, 96) for _ in range(2)]
        R0, E0 = bufs[0:4], bufs[4:8]
        PP = [t.bitcast(BF).rearrange("p (w a n) -> p w a n", w=2, a=3)
              for t in (ra(3 * HW_, 96), ra(3 * HW_, 96), PX[0:96, :])]
        XD = [XI[:, i, :, :].rearrange("p a c -> p (a c)")[:, 0:512] for i in range(2)] + [ra(512) for _ in range(6)]
        xpw = ra(512, 96).rearrange("p (m k c) -> p m k c", m=2, k=2)
        dtw = WD[:, :].rearrange("p (k c) -> p k c", k=2)
        dma(("f.w", 0), "w0", xpw, A["xpw"])
        for j in range(2):
            dma(("f.xcout", 0), "w1", xcd[par, j], C1[:, j, :])
        yield 5 * W_CHAIN
        wait(PE, ("f.w", 0))

        def project(p):
            kk, v_ = divmod(p, 8)
            q4, m_ = divmod(v_, 2)
            if m_:
                return
            for i in (2 * q4, 2 * q4 + 1):
                n_ = 8 * kk + i
                cs_ = slice(i * 512, (i + 1) * 512)
                n, pb = bank()
                for m in range(2):
                    x_ = C1[:, m, cs_] if kk == 0 else C1T[:, m, 8 * i:8 * i + 8, :]
                    t = mm(pb[:, :], xpw[:, m, kk, :], x_, m == 0, m == 1)
                mark(("f.xp", n_), PE.inc(t))
                wait(AC, ("f.xp", n_), ("f.xdout", n_ - 8), ("f.dt", 8 * (kk - 1) + 2 * (i // 2) + 1))
                mark(("f.xd", n_), act(XD[i], pb[:, :], ACT.Copy))
                emptied(n, done["f.xd", n_])
                yield 1.7
                wait(SP, ("f.xd", n_))
                dma(("f.xdout", n_), f"xd{i}", bcd[par, kk::2, :, cs_], XD[i][64:128, :])

        def steps(p):
            kk, v_ = divmod(p, 8)
            q4, m = divmod(v_, 2)
            wait(AC, ("f.p2", 2 * (p - 2) + 1))
            for i in range(2):
                t_ = 2 * q4 + i
                o = slice(i * 512, (i + 1) * 512)
                wait(PE, ("f.xd", 8 * kk + t_))
                for h_ in range(2):
                    u = 2 * p + h_
                    bias = vec("dtb1", (kk + 2 * h_) * 2 + m)
                    n, pb = bank()
                    mark(("f.dt", p), PE.inc(mm(pb[0:96, :], dtw[32 * h_:32 * h_ + 6, kk, m * 96:(m + 1) * 96],
                                                XD[t_][32 * h_:32 * h_ + 6, :], True, True)))
                    wait(AC, ("f.dt", p))
                    mark(("f.abs", u), act(E0[u % 4][:, o], pb[0:96, :], ACT.Abs, bias=bias))
                    emptied(n, act(R0[u % 4][:, o], pb[0:96, :], ACT.Relu, bias=bias))
                    mark(("f.relu", u), done["emptied", n])
                    yield 0.9
            for u in (2 * p, 2 * p + 1):
                wait(AC, ("f.abs", u))
                mark(("f.exp", u), act(E0[u % 4], E0[u % 4], ACT.Exp, scale=-1.0))
                yield 0.5

        def split(p):
            kk, v_ = divmod(p, 8)
            q4, m = divmod(v_, 2)
            hs = slice(q4 * HW_, (q4 + 1) * HW_)
            pair = (2 * p, 2 * p + 1)
            for u in pair:
                wait(AC, ("f.exp", u))
                mark(("f.ln", u), act(E0[u % 4], E0[u % 4], ACT.Ln, bias=ONE[0:96, 0:1]))
            yield 0.5
            for u in pair:
                r_, e_, pp = R0[u % 4], E0[u % 4], PP[u % 3]
                wait(DV, ("f.ln", u), ("f.relu", u))
                mark(("f.sum", u), tt(r_, r_, e_, ADD))
                wait(DV, ("f.sum", u), ("f.pout", u - 3))
                mark(("f.p0", 2 * u), DV.inc(nc.vector.tensor_copy(pp[:, 0, 0, :], r_)))
                if kk == 0:
                    mark(("f.du", u), tt(e_, r_, C1[:, m, hs], MUL))
                else:
                    mark(("f.du", u), tt(e_.rearrange("p (w h) -> p w h", h=64), r_.rearrange("p (w h) -> p w h", h=64),
                                         C1T[:, m, q4 * 16:(q4 + 1) * 16, :], MUL))
                wait(AC, ("f.du", u), ("f.pout", u - 3))
                mark(("f.p0", 2 * u + 1), act(pp[:, 1, 0, :], e_, ACT.Copy))
                yield 1
            for u in pair:
                r_, e_, pp = R0[u % 4], E0[u % 4], PP[u % 3]
                for w, x_ in ((0, r_), (1, e_)):
                    v2 = 2 * u + w
                    wait(DV, ("f.p0", v2), ("f.du", u))
                    mark(("f.x1", v2), tt(x_, x_, pp[:, w, 0, :], SUB))
                    wait(AC, ("f.x1", v2))
                    mark(("f.p1", v2), act(pp[:, w, 1, :], x_, ACT.Copy))
                    wait(PO, ("f.p1", v2))
                    mark(("f.x2", v2), ptt(pp[:, w, 2, :], x_, pp[:, w, 1, :], SUB))
                    yield 0.5
                mark(("f.p2", u), done["f.x2", 2 * u + 1])
                wait(SP, ("f.p2", u))
                for a_ in range(3):
                    dma(("f.pout", u), f"pp{u % 3}", ptd[par, kk + 2 * (u % 2), 3 * m:3 * m + 3, a_ * 32:a_ * 32 + 32, :, hs],
                        pp[:, :, a_, :])
        yield from scaled(W_F, woven(16, idle, project, steps, split))

    def scan(b, par):
        units = [(k, c, d, g) for k in range(4) for c in (range(4) if k < 2 else range(3, -1, -1))
                 for d in range(6) for g in range(4)]
        N = len(units)

        def fetch_bc(v):
            k, c, _, _ = units[24 * v]
            cs_ = slice(c * 1024, (c + 1) * 1024)
            wait(SP, ("S.mulC", 24 * (v - NBR) + 23))
            for w in range(2):
                dma(("S.bc", v), f"Sbc{v % NBR}", BR[:, v % NBR, w, :],
                    bcd[par, k, w * 16:w * 16 + 16, cs_].unsqueeze(0).to_broadcast([8, 16, 1024]))

        def fetch_pt(v):
            k, c, d, _ = units[4 * v]
            wait(SP, ("S.PU", 4 * (v - NPT) + 3))
            dma(("S.pt", v), f"Spt{v % NPT}", PT[:, v % NPT, :, :], ptd[par, k, d, :, :, c * 1024:(c + 1) * 1024])

        def expand(u, q, which, out, key):
            t = mm(out, SEL[:, units[u][3], :], PT[:, (u // 4) % NPT, which, q * 512:(q + 1) * 512], True, True)
            mark(key, PE.inc(t))

        def decay(u, q):
            k, c, d, g = units[u]
            wait(PE, ("S.pt", u // 4), ("S.exp", 1 - q, u - 1 + q))
            expand(u, q, 0, PD[:, :], ("S.PD", q, u))
            ai = k * 24 + d * 4 + g
            wait(AC, ("S.PD", q, u), ("S.scan", u - NA))
            mark(("S.exp", q, u), act(dA[:, u % NA, q * 512:(q + 1) * 512], PD[:, :], ACT.Exp, scale=A1[:, ai:ai + 1]))

        def drive(u):
            wait(PE, ("S.pt", u // 4), ("S.mulB", u - 1))
            for q in range(2):
                expand(u, q, 1, PU[:, q * 512:(q + 1) * 512], ("S.PU", u))
            wait(DV, ("S.PU", u), ("S.bc", u // 24), ("S.mulC", u - NH), ("S.last", (u - NH) | 1 if u >= NH else -1))
            mark(("S.mulB", u), tt(H[:, u % NH, :], PU[:, :], BR[:, (u // 24) % NBR, 0, :], MUL))

        def scan_(u):
            k, c, d, g = units[u]
            gi = d * 4 + g
            first = c == (0 if k < 2 else 3)
            h, a_ = H[:, u % NH, :], dA[:, u % NA, :]
            wait(DV, ("S.exp", 1, u), ("S.mulB", u))
            if not first:
                wait(DV, ("S.last", (u - 24) | 1))
            init = 0.0 if first else CR[:, gi:gi + 1]
            if k >= 2:
                h, a_ = h[:, ::-1], a_[:, ::-1]
            mark(("S.scan", u), DV.inc(nc.vector.tensor_tensor_scan(h, a_, h, init, MUL, ADD)))
            if u % 2 == 1:
                s0 = (u - 1) % NH
                wait(AC, ("S.scan", u))
                mark(("S.last", u), act(CR[:, gi - 1:gi + 1], H[:, s0:s0 + 2, 1023 if k < 2 else 0], ACT.Copy))
            wait(PO, ("S.scan", u), ("S.sum", u - NHC))
            mark(("S.mulC", u), ptt(HC[:, u % NHC, :], H[:, u % NH, :], BR[:, (u // 24) % NBR, 1, :], MUL))

        def total(u):
            k, c, d, g = units[u]
            v = u // 4
            wait(PE, ("S.mulC", u), ("S.y", v - 1))
            for q in range(4):
                t = mm(PY[32 * q:32 * q + 32, :], RED[:, g, :], HC[:, u % NHC, q * 256:(q + 1) * 256], g == 0, g == 3)
            mark(("S.sum", u), PE.inc(t))
            if g == 3:
                wait(AC, ("S.sum", u), ("S.yout", v - 2))
                mark(("S.y", v), act(YS[:, v % 2, :], PY[:, :], ACT.Copy))

        def put(v):
            k, c, d, _ = units[4 * v]
            wait(SP, ("S.y", v))
            dma(("S.yout", v), f"Syo{v % 2}", yd[par, k, d, c], YS[:, v % 2, :])

        fetch_bc(0)
        fetch_pt(0)
        fetch_bc(1)
        fetch_pt(1)
        LAG = 3
        decay(0, 0)
        decay(0, 1)
        for u in range(N + LAG + 1):
            if 1 <= u <= N:
                scan_(u - 1)
            yield 1
            if u < N:
                drive(u)
            if u + 1 < N:
                decay(u + 1, 0)
            yield 1
            if LAG <= u < N + LAG:
                total(u - LAG)
            if u + 1 < N:
                decay(u + 1, 1)
            if u % 4 == 0 and NPT <= u // 4 + 1 < N // 4:
                fetch_pt(u // 4 + 1)
            if u % 4 == LAG % 4 and 4 < u < N + LAG:
                put((u - LAG) // 4 - 1)
            if u % 24 == LAG and (v := u // 24 + 1) >= NBR and 24 * v < N:
                fetch_bc(v)
            yield 1
        put(N // 4 - 1)

    def finish(b, par):
        phase()
        ra, rb = Cutter(RA, 3 * PADN), Cutter(RB, 2 * L)
        XM = ra(2 * L, 96).rearrange("p (j l) -> p j l", j=2)
        VR = ra(L, 96)
        Y13 = rb(2 * L, 96).rearrange("p (j l) -> p j l", j=2)
        Y13v = RB[0:96, 0:2 * L].rearrange("p (j w h) -> p j h w", j=2, w=64)

        def halves(k, j, cc):
            return [yd[par, k, 3 * j + g, cc].rearrange("c (q r) n -> r (c q) n", q=4) for g in range(3)]

        for j in range(2):
            for g in range(3):
                for (k, dst) in ((1, XM), (3, Y13)):
                    dma((f"g.y{k}", 0), f"w{k}", dst[32 * g:32 * g + 32, j, :].rearrange("p (a n) -> p a n", n=256),
                        yd[par, k, 3 * j + g].rearrange("c (q r) n -> r (c q) n", q=4))
        yield 25 * W_CHAIN
        for i in range(8):
            wait(PO, ("g.y1", 0), ("g.y3", 0))
            s_ = slice(i * 1024, (i + 1) * 1024)
            mark(("g.y13", 0), ptt(RB[0:96, s_], RB[0:96, s_], RA[0:96, s_], ADD))
            yield 3 * W_CHAIN
        BA, BB = B2, X2

        def gload(i):
            cs_ = slice(i * 512, (i + 1) * 512)
            wait(SP, ("g.xm", i - 2), ("g.mean", i - 2), ("g.y02", i - 1), ("g.d", i - 1))
            for k, dst, nm in ((0, XT[:, i % 2], f"xt{i % 2}"), (2, BA, "b2")):
                for j in range(2):
                    for g in range(3):
                        src = yd[par, k, 3 * j + g, i // 2].rearrange("(q r) n -> r q n", q=4)[:, 2 * (i % 2):2 * (i % 2) + 2, :]
                        dma((f"g.y{k}", i), nm, dst[32 * g:32 * g + 32, j, :].rearrange("p (a n) -> p a n", n=256), src)
            dma(("g.xc", i), "x2", BB[:, :, :], xcd[par, :, :, cs_].rearrange("j p n -> p j n"))
            yield 0

        def total(i):
            cs_ = slice(i * 512, (i + 1) * 512)
            a_ = XT[:, i % 2]
            wait(DV, ("g.y0", i), ("g.y2", i), ("g.y13", 0))
            mark(("g.y02", i), tt(a_, a_, BA[:, :, :], ADD))
            wait(DV, ("g.y02", i))
            for j in range(2):
                v = a_[:, j, :].rearrange("p (h w) -> p h w", h=8)
                mark(("g.yall", i), tt(v, v, Y13v[:, j, 8 * i:8 * i + 8, :], ADD))
            wait(DV, ("g.yall", i), ("g.xc", i))
            for j in range(2):
                mark(("g.d", i), stt(a_[:, j, :], BB[:, j, :], DV0[0:96, 30 + j:31 + j], a_[:, j, :], MUL, ADD))
            yield 1

        def mean(i):
            cs_ = slice(i * 512, (i + 1) * 512)
            a_ = XT[:, i % 2]
            n, pb = bank()
            wait(PE, ("g.d", i))
            for j in range(2):
                t = mm(pb[0:96, :], M192[:, :], a_[:, j, :], j == 0, j == 1)
            mark(("g.mean", i), PE.inc(t))
            wait(DV, ("g.mean", i), ("g.d", i))
            for j in range(2):
                mark(("g.xm", i), tt(XM[:, j, cs_], a_[:, j, :], pb[0:96, :], SUB))
            emptied(n, done["g.xm", i])
            yield 1
            wait(AC, ("g.xm", i), ("g.var", i - 1))
            for j in range(2):
                mark(("g.sq", i), act(T0[0:96, j, :], XM[:, j, cs_], ACT.Square))
            yield 1

        def var(i):
            cs_ = slice(i * 512, (i + 1) * 512)
            n, pb = bank()
            wait(PE, ("g.sq", i))
            for j in range(2):
                t = mm(pb[0:96, :], M192[:, :], T0[0:96, j, :], j == 0, j == 1)
            mark(("g.var", i), PE.inc(t))
            wait(AC, ("g.var", i))
            mark(("g.vr", i), act(VR[:, cs_], pb[0:96, :], ACT.Copy))
            emptied(n, done["g.vr", i])
            yield 1
        yield from woven(8, gload, total, mean, var)
        wait(AC, ("g.vr", 7))
        mark(("g.ln", 0), act(VR, VR, ACT.Ln, bias=ONE[0:96, 1:2]))
        yield 6 * W_CHAIN
        wait(AC, ("g.ln", 0))
        mark(("g.rstd", 0), act(VR, VR, ACT.Exp, scale=-0.5))
        yield 6 * W_CHAIN
        ov = A["out"][b].rearrange("(i q p) c -> i p q c", q=4, p=128)
        wait(DV, ("g.rstd", 0), ("g.xm", 7))
        ZB = [rb_ for rb_ in (RB[0:96, 0:1024], RB[0:96, 1024:2048])]
        XB = [rb_ for rb_ in (RB[0:96, 2048:3072], RB[0:96, 3072:4096])]
        LB = [rb_ for rb_ in (RB[0:96, 4096:4608], RB[0:96, 4608:5120])]
        wait(SP, ("g.yall", 7), ("g.mean", 7), ("g.d", 7))

        def hload(i):
            cs_ = slice(i * 512, (i + 1) * 512)
            wait(SP, ("h.gate", 2 * (i - 2) + 1), ("h.mm", 2 * (i - 2) + 1))
            dma(("h.z", i), f"hz{i % 2}", ZB[i % 2].rearrange("p (j n) -> p j n", j=2),
                zd[par, :, :, cs_].rearrange("j p n -> p j n"))
            dma(("h.x", i), f"hx{i % 2}", XB[i % 2].rearrange("p (j n) -> p j n", j=2),
                x1d[par, :, :, cs_].rearrange("j p n -> p j n"))
            dma(("h.l", i), f"hl{i % 2}", LB[i % 2], xld[par, :, cs_])
            yield 0

        def gates(i):
            cs_ = slice(i * 512, (i + 1) * 512)
            for j in range(2):
                m = 2 * i + j
                o = XT[:, i % 2, j, :]
                wait(DV, ("h.mm", 2 * (i - 2) + 1))
                mark(("h.n", m), tt(o, XM[:, j, cs_], VR[:, cs_], MUL))
                wait(AC, ("h.n", m))
                mark(("h.g", m), act(o, o, ACT.Identity, bias=vec("onb", j), scale=vec("ong", j)))
                yield 1
                wait(DV, ("h.g", m), ("h.z", i))
                mark(("h.gate", m), tt(o, o, ZB[i % 2][:, j * 512:(j + 1) * 512], MUL))

        def final(i):
            wait(PE, ("h.gate", 2 * i + 1), ("h.x", i), ("h.l", i))
            for q2 in range(2):
                n, pb = bank()
                for q in range(2):
                    o = pb[:, q * 192:(q + 1) * 192]
                    s_ = slice((q2 * 2 + q) * 128, (q2 * 2 + q + 1) * 128)
                    s1 = slice(512 + (q2 * 2 + q) * 128, 512 + (q2 * 2 + q + 1) * 128)
                    mm(o, XT[:, i % 2, 0, s_], WP[:, 0:192], True, False)
                    mm(o, XT[:, i % 2, 1, s_], WP[:, 192:384], False, False)
                    mm(o, LB[i % 2][:, s_], PERM[:, 0:192], False, False)
                    mm(o, XB[i % 2][:, s_], PERM[:, 384:576], False, False)
                    t = mm(o, XB[i % 2][:, s1], PERM[:, 576:768], False, True)
                mark(("h.mm", 2 * i + q2), PE.inc(t))
                wait(AC, ("h.mm", 2 * i + q2), ("h.out", i - 2))
                emptied(n, act(XI[:, i % 2, 2 * q2:2 * q2 + 2, :], pb[:, 0:384].rearrange("p (q c) -> p q c", q=2),
                               ACT.Copy))
                yield 3.2
            wait(SP, ("emptied", n))
            dma(("h.out", i), f"xi{i % 2}", ov[i], XI[:, i % 2, :, :])
        yield from woven(8, hload, gates, final)

    def reset():
        for n in lanes:
            if count[n]:
                nc.sync.wait_ge(lanes[n], count[n])
        nc.all_engine_barrier()
        for s_ in [e.sem for e in engines] + list(lanes.values()):
            nc.gpsimd.sem_clear(s_)
        nc.all_engine_barrier()
        done.clear()
        bank_no[0] = 0
        for e in engines:
            e.n = 0
        for n in count:
            count[n] = 0

    def chain(*gens):
        for g in gens:
            yield from g

    def run(gen):
        t = 0
        for c in gen:
            t += c
        return t

    def beside(s_gen, d_gen, total_):
        at, n = 0.0, 0
        spent = 0.0
        for _ in s_gen:
            n += 1
            while at < total_ * n / 1155:
                c = next(d_gen, None)
                if c is None:
                    at = float("inf")
                    break
                at += c
                spent += c
        spent += run(d_gen)
        return spent

    setup()
    reset()
    tot = run(chain(layer0(0, 0), layer1(0, 0)))
    reset()
    PRE, FIN = tot, 135.0
    beside(scan(0, 0), chain(layer0(1, 1), layer1(1, 1)), PRE)
    reset()
    if NB > 2:
        with nc.Fori(1, NB - 2, 2) as i:
            for o in range(2):
                p = (1 + o) % 2
                beside(scan(i + o, p), chain(finish(i + (o - 1), 1 - p), layer0(i + (o + 1), 1 - p),
                                             layer1(i + (o + 1), 1 - p)), PRE + FIN)
                reset()
    beside(scan(NB - 1, 1), finish(NB - 2, 0), FIN)
    reset()
    run(finish(NB - 1, 1))
    reset()


def _consts():
    c = np.zeros((128, NC_), np.float32)

    def put(name, a):
        x, _ = CCOL[name]
        c[:a.shape[0], x:x + a.shape[1]] = a
    put("ident", np.eye(128, dtype=np.float32))
    i = np.arange(128)
    put("tri", (i[:, None] <= i[None, :]).astype(np.float32))
    put("ones", np.ones((128, 128), np.float32))
    red = np.zeros((128, 4, 32), np.float32)
    sel = np.zeros((96, 4, 128), np.float32)
    for g in range(4):
        for d in range(8):
            for n in range(16):
                red[d * 16 + n, g, g * 8 + d] = 1
                for part in range(3):
                    sel[part * 32 + g * 8 + d, g, d * 16 + n] = 1
    put("red", red.reshape(128, 128))
    put("sel", sel.reshape(96, 512))
    put("neg", np.where(i[None, :] >= i[:, None], 0.0, -1e30).astype(np.float32))
    one3 = np.zeros((96, 32), np.float32)
    one3[0:3] = 1
    put("one3", one3)
    perm = np.zeros((96, 768), np.float32)
    for j in range(96):
        perm[j, 2 * j] = 1
        perm[j, 192 + 2 * j + 1] = 1
        perm[j, 384 + j] = 1
        perm[j, 576 + 96 + j] = 1
    put("perm", perm)
    return c


def _layouts(a, NB):
    def cols(x, P):
        return np.asarray(x).reshape(-1, P).T
    v = np.zeros((128, NV), np.float32)

    def put(name, x):
        lo, hi_ = VCOL[name]
        assert x.shape[1] == hi_ - lo, name
        v[:x.shape[0], lo:hi_] = x
    p0, p1 = "L0_conv_", "L1_conv_"
    put("cb", cols(a[p0 + "conv_b"], 128))
    put("ds0", cols(np.repeat(a[p0 + "Ds"], 64), 128))
    put("b1", cols(a[p0 + "b1"], 128))
    put("b2", cols(a[p0 + "b2"], 96))
    put("alog0", np.broadcast_to(a[p0 + "A_logs"], (128, 12)))
    put("dtb0", np.broadcast_to(a[p0 + "dt_bias"], (128, 12)))
    for i in (1, 2, 3):
        put(f"bn{i}", np.stack([a[f"{p1}bn{i}_{q}"] for q in "gbmv"], 1))
        put(f"c{i}b", cols(a[f"{p1}conv{i}_b"], 96))
    put("lng", cols(a[p1 + "ln_g"], 96))
    put("lnb", cols(a[p1 + "ln_b"], 96))
    put("cdb", cols(a[p1 + "conv2d_b"], 96))
    put("dtb1", cols(a[p1 + "dt_proj_b"], 96))
    put("ds1", cols(a[p1 + "Ds"], 96))
    put("ong", cols(a[p1 + "out_norm_g"], 96))
    put("onb", cols(a[p1 + "out_norm_b"], 96))
    put("alog1", a[p1 + "A_logs"].reshape(4, 24, 8, 16).transpose(2, 3, 0, 1).reshape(128, 96))
    put("w0", a[p0 + "conv_w"].reshape(3, 128, 9).transpose(1, 0, 2).reshape(128, 27))
    put("w1", a[p1 + "conv2d_w"].reshape(9, 2, 96).transpose(2, 1, 0).reshape(96, 18))
    o = {"vecs": v, "consts": _consts()}
    o["x"] = a["x"].reshape(8, L, 192)[:NB]
    o["win"] = a[p0 + "W_in"].T.reshape(2, 96, 768).transpose(1, 0, 2)
    xp = a[p0 + "x_proj_weight"]
    xp = np.concatenate([xp[:, 32:64], xp[:, 0:32], xp[:, 64:70]], 1)
    o["wxp0"] = xp.transpose(2, 0, 1).reshape(3, 128, 2, 70).transpose(1, 0, 2, 3)
    o["h0"] = a[p0 + "init_states"].transpose(2, 0, 1).reshape(32, 768)
    o["wout0"] = a[p0 + "W_out"].T.reshape(3, 128, 192).transpose(1, 0, 2)
    o["w1"] = a[p0 + "W1"].T.reshape(2, 96, 768).transpose(1, 0, 2)
    o["w2"] = a[p0 + "W2"].T.reshape(6, 128, 192).transpose(1, 0, 2)
    o["c1"] = a[p1 + "conv1_w"].reshape(9, 96, 96).transpose(1, 0, 2)
    o["c2"] = a[p1 + "conv2_w"].reshape(9, 96, 96).transpose(1, 0, 2)
    o["c3"] = a[p1 + "conv3_w"].reshape(96, 96)
    o["wip"] = a[p1 + "in_proj_w"].T
    xp = a[p1 + "x_proj_w"].transpose(2, 0, 1).reshape(2, 96, 4, 38).transpose(1, 0, 2, 3)
    xq = np.zeros((96, 2, 2, 128), np.float32)
    for i in range(2):
        xq[..., 32 * i:32 * i + 6] = xp[:, :, 2 * i:2 * i + 2, 0:6]
        xq[..., 64 + 32 * i:96 + 32 * i] = xp[:, :, 2 * i:2 * i + 2, 6:38]
    o["xpw"] = xq
    o["dtw"] = a[p1 + "dt_proj_w"].transpose(2, 0, 1)
    wop = np.zeros((96, 2, 192), np.float32)
    wop[:, :, 1::2] = a[p1 + "out_proj_w"].T.reshape(2, 96, 96).transpose(1, 0, 2)
    o["wop"] = wop.reshape(96, 384)
    return {k: np.ascontiguousarray(x, dtype=np.float32) for k, x in o.items()}


def kernel(**inputs):
    import concourse.bacc as _bacc
    from concourse import mybir as _mybir
    from concourse.bass_utils import run_bass_kernel_spmd as _run

    NB = 8
    nc = _bacc.Bacc("TRN2", target_bir_lowering=False, num_devices=1)
    arrays = {f"in_{k}": x for k, x in _layouts({k: np.asarray(x) for k, x in inputs.items()}, NB).items()}
    A = {k[3:]: nc.dram_tensor(k, x.shape, _mybir.dt.from_np(x.dtype), kind="ExternalInput").ap()
         for k, x in arrays.items()}
    A["out"] = nc.dram_tensor("out_0", (NB, L, 192), F32, kind="ExternalOutput").ap()
    program(nc, A, NB)
    r = _run(nc, [arrays], core_ids=[0])
    return r.results[0]["out_0"].reshape(NB, 64, 64, 192)
```
